# Optimizing a Trainium2 kernel written in Bass

```python
import numpy as np
import jax
import jax.numpy as jnp

def _softmax(x, axis=-1):
    return jax.nn.softmax(x, axis=axis)

def _gelu(x):
    return jax.nn.gelu(x, approximate=True)

def _silu(x):
    return jax.nn.silu(x)

def _sigmoid(x):
    return jax.nn.sigmoid(x)

def _layernorm(x, axis=-1, eps=1e-05):
    m = jnp.mean(x, axis=axis, keepdims=True)
    v = jnp.var(x, axis=axis, keepdims=True)
    return (x - m) / jnp.sqrt(v + eps)

def _scatter_add(tgt, idx, src, axis=0):
    return tgt.at[idx].add(src)

def _segment_sum(src, seg, n):
    return jax.ops.segment_sum(src, seg, n)
kernel_name = 'mk_flamingo_gated_d2_seqx_r8_ea9c28'

def setup_inputs(seed: int=0):
    np.random.seed(seed)
    _w = jnp.asarray

    def _rec_inputs():
        import jax
        import jax.numpy as jnp
        _rk = jax.random.key(seed)
        x = 4.136e-05 + 0.9999 * jax.random.normal(jax.random.fold_in(_rk, 1), (4, 256, 256), jnp.float32)
        _lenS = 256 - jax.random.randint(jax.random.fold_in(_rk, 7), (4,), 0, max(1, 256 // 4) + 1, jnp.int32)
        _lenS2 = 256 - jax.random.randint(jax.random.fold_in(_rk, 8), (4,), 0, max(1, 256 // 4) + 1, jnp.int32)
        _ctx_1024P = jax.random.normal(jax.random.fold_in(_rk, 11), (4, 16, 128), jnp.float32)
        _ctx_1024c = jax.random.dirichlet(jax.random.fold_in(_rk, 511), 0.3 * jnp.ones((16,), jnp.float32), (4, 256))
        _ctx_1024t = jnp.einsum('bsk,bkd->bsd', _ctx_1024c, _ctx_1024P)
        _ctx_1024t = _ctx_1024t * jax.lax.rsqrt(jnp.mean(jnp.square(_ctx_1024t)) + 1e-12) * 0.953939
        ctx_1024 = -0.000292821 + 1.00034 * (_ctx_1024t + 0.3 * jax.random.normal(jax.random.fold_in(_rk, 611), (4, 256, 128), jnp.float32))
        _g = jax.random.normal(jax.random.fold_in(_rk, 9001), (2, 2), jnp.float32)
        _g = jnp.sign(_g) * jnp.maximum(jnp.abs(_g), 1.0) + (_g == 0) * 1.0
        g_xattn = _g[0]
        g_ffn = _g[1]
        return (x, ctx_1024, g_xattn, g_ffn)
    x, ctx_1024, g_xattn, g_ffn = _rec_inputs()

    def _L0_xattn_setup():
        import jax, jax.numpy as jnp
        import numpy as np
        import math
        B, L, DM = (2, 256, 128)
        DS, DC, EXP = (16, 4, 2)
        DI = EXP * DM
        DR = math.ceil(DM / 16)
        DT_MIN, DT_MAX, DT_FLOOR = (0.001, 0.1, 0.0001)

        def _ssm_forward(hidden_states, z, in_proj_w, conv_w, conv_b, x_proj_w, dt_proj_w, dt_proj_b, A_log, D):
            b = hidden_states.shape[0]
            x = jnp.einsum('ed,bld->bel', in_proj_w, hidden_states)
            xp = jnp.pad(x, ((0, 0), (0, 0), (DC - 1, 0)))
            xc = jax.lax.conv_general_dilated(xp, conv_w[:, None, :], window_strides=(1,), padding='VALID', dimension_numbers=('NCH', 'OIH', 'NCH'), feature_group_count=DI)
            u = jax.nn.silu(xc + conv_b[None, :, None])
            x_dbl = jnp.einsum('ke,bel->bkl', x_proj_w, u)
            dt_lo = x_dbl[:, :DR]
            Bm = x_dbl[:, DR:DR + DS]
            Cm = x_dbl[:, DR + DS:]
            delta = jax.nn.softplus(jnp.einsum('er,brl->bel', dt_proj_w, dt_lo) + dt_proj_b[None, :, None])
            A = -jnp.exp(A_log)

            def step(state, xs):
                d_t, B_t, C_t, u_t = xs
                dA = jnp.exp(d_t[..., None] * A)
                state = state * dA + (d_t * u_t)[..., None] * B_t[:, None, :]
                y_t = jnp.einsum('ben,bn->be', state, C_t)
                return (state, y_t)
            xs = (jnp.moveaxis(delta, -1, 0), jnp.moveaxis(Bm, -1, 0), jnp.moveaxis(Cm, -1, 0), jnp.moveaxis(u, -1, 0))
            state0 = jnp.zeros((b, DI, DS), delta.dtype)
            _, ys = jax.lax.scan(step, state0, xs)
            y = jnp.moveaxis(ys, 0, -1)
            y = y + D[None, :, None] * u
            y = y * jax.nn.silu(z)
            return jnp.swapaxes(y, 1, 2)
        key = jax.random.key(seed)
        ks = jax.random.split(key, 8)
        hidden_states = jax.random.normal(ks[0], (B, L, DM), jnp.float32)
        z = jax.random.normal(ks[1], (B, DI, L), jnp.float32)
        in_proj_w = jax.random.normal(ks[2], (DI, DM), jnp.float32) * DM ** (-0.5)
        conv_w = jax.random.normal(ks[3], (DI, DC), jnp.float32) * DC ** (-0.5)
        conv_b = jnp.zeros((DI,), jnp.float32)
        x_proj_w = jax.random.normal(ks[4], (DR + 2 * DS, DI), jnp.float32) * DI ** (-0.5)
        dt_std = DR ** (-0.5)
        dt_proj_w = jax.random.uniform(ks[5], (DI, DR), jnp.float32, -dt_std, dt_std)
        dt = jnp.exp(jax.random.uniform(ks[6], (DI,), jnp.float32) * (math.log(DT_MAX) - math.log(DT_MIN)) + math.log(DT_MIN))
        dt = jnp.clip(dt, DT_FLOOR)
        dt_proj_b = dt + jnp.log(-jnp.expm1(-dt))
        A_log = jnp.log(jnp.broadcast_to(jnp.arange(1, DS + 1, dtype=jnp.float32), (DI, DS)))
        D = jnp.ones((DI,), jnp.float32)
        return dict(hidden_states=hidden_states, z=z, in_proj_w=in_proj_w, conv_w=conv_w, conv_b=conv_b, x_proj_w=x_proj_w, dt_proj_w=dt_proj_w, dt_proj_b=dt_proj_b, A_log=A_log, D=D)
    _L0_xattn_all = _L0_xattn_setup()
    _L0_xattn_in = {k: v for k, v in _L0_xattn_all.items() if k in ('in_proj_w', 'conv_w', 'conv_b', 'x_proj_w', 'dt_proj_w', 'dt_proj_b', 'A_log', 'D')}
    del _L0_xattn_all

    def _L0_ffn_setup():
        import jax, jax.numpy as jnp
        import numpy as np
        TOPK = 2
        HID, INTER, E, SHARED_INTER = (256, 176, 14, 352)
        key = jax.random.key(seed)
        ks = jax.random.split(key, 11)
        s = 0.02
        return {'x': jax.random.normal(ks[0], (4, 64, HID), jnp.float32), 'gate_w': jax.random.normal(ks[1], (E, HID), jnp.float32) * s, 'cls_w': jax.random.normal(ks[2], (E, HID), jnp.float32) * s, 'extra_scale': jax.random.normal(ks[3], (E,), jnp.float32) * 0.1, 'extra_bias': jax.random.normal(ks[4], (E,), jnp.float32) * 0.01, 'wg': jax.random.normal(ks[5], (E, INTER, HID), jnp.float32) * s, 'wu': jax.random.normal(ks[6], (E, INTER, HID), jnp.float32) * s, 'wd': jax.random.normal(ks[7], (E, HID, INTER), jnp.float32) * s, 'sg': jax.random.normal(ks[8], (SHARED_INTER, HID), jnp.float32) * s, 'su': jax.random.normal(ks[9], (SHARED_INTER, HID), jnp.float32) * s, 'sd': jax.random.normal(ks[10], (HID, SHARED_INTER), jnp.float32) * s}
    _L0_ffn_all = _L0_ffn_setup()
    _L0_ffn_in = {k: v for k, v in _L0_ffn_all.items() if k in ('gate_w', 'cls_w', 'extra_scale', 'extra_bias', 'wg', 'wu', 'wd', 'sg', 'su', 'sd')}
    del _L0_ffn_all

    def _L1_xattn_setup():
        import jax, jax.numpy as jnp
        import numpy as np
        B_, L_, D_MODEL = (4, 256, 128)
        D_STATE, D_CONV, EXPAND = (16, 4, 2)
        D_INNER = EXPAND * D_MODEL
        DT_RANK = (D_MODEL + 15) // 16

        def silu(x):
            return x * jax.nn.sigmoid(x)
        key = jax.random.key(seed)
        ks = jax.random.split(key, 10)
        f32 = jnp.float32
        hidden_states = jax.random.normal(ks[0], (B_, L_, D_MODEL), dtype=f32)
        z = jax.random.normal(ks[1], (B_, D_INNER, L_), dtype=f32)
        in_proj_w = jax.random.normal(ks[2], (D_INNER, D_MODEL), dtype=f32) * 0.02
        conv_w = jax.random.normal(ks[3], (D_INNER, 1, D_CONV), dtype=f32) * 0.1
        conv_b = jax.random.normal(ks[4], (D_INNER,), dtype=f32) * 0.02
        x_proj_w = jax.random.normal(ks[5], (DT_RANK + 2 * D_STATE, D_INNER), dtype=f32) * 0.02
        dt_proj_w = jax.random.uniform(ks[6], (D_INNER, DT_RANK), dtype=f32, minval=-DT_RANK ** (-0.5), maxval=DT_RANK ** (-0.5))
        dt = jnp.exp(jax.random.uniform(ks[7], (D_INNER,), dtype=f32, minval=np.log(0.001), maxval=np.log(0.1)))
        dt_proj_b = jnp.log(jnp.expm1(dt))
        A_log = jnp.log(jnp.broadcast_to(jnp.arange(1, D_STATE + 1, dtype=f32), (D_INNER, D_STATE)))
        D = jnp.ones((D_INNER,), f32)
        return {'hidden_states': hidden_states, 'z': z, 'in_proj_w': in_proj_w, 'conv_w': conv_w, 'conv_b': conv_b, 'x_proj_w': x_proj_w, 'dt_proj_w': dt_proj_w, 'dt_proj_b': dt_proj_b, 'A_log': A_log, 'D': D}
    _L1_xattn_all = _L1_xattn_setup()
    _L1_xattn_in = {k: v for k, v in _L1_xattn_all.items() if k in ('in_proj_w', 'conv_w', 'conv_b', 'x_proj_w', 'dt_proj_w', 'dt_proj_b', 'A_log', 'D')}
    del _L1_xattn_all

    def _L1_ffn_setup():
        import jax, jax.numpy as jnp
        import numpy as np
        DIM = 256
        EXPERT_DIM = 128
        N_EXPERTS = 16
        TOPK = 2
        N_SHARED = 1
        B, T = (4, 256)
        key = jax.random.key(seed)
        ks = jax.random.split(key, 9)
        s = 0.02
        return {'x': jax.random.normal(ks[0], (B, T, DIM), jnp.float32), 'router_w': jax.random.normal(ks[1], (N_EXPERTS, DIM), jnp.float32) * s, 'router_bias': jnp.zeros((N_EXPERTS,), jnp.float32), 'Wu': jax.random.normal(ks[2], (N_EXPERTS, DIM, EXPERT_DIM), jnp.float32) * s, 'Wg': jax.random.normal(ks[3], (N_EXPERTS, DIM, EXPERT_DIM), jnp.float32) * s, 'Wd': jax.random.normal(ks[4], (N_EXPERTS, EXPERT_DIM, DIM), jnp.float32) * s, 'Su': jax.random.normal(ks[5], (N_SHARED, DIM, EXPERT_DIM * TOPK), jnp.float32) * s, 'Sg': jax.random.normal(ks[6], (N_SHARED, DIM, EXPERT_DIM * TOPK), jnp.float32) * s, 'Sd': jax.random.normal(ks[7], (N_SHARED, EXPERT_DIM * TOPK, DIM), jnp.float32) * s}
    _L1_ffn_all = _L1_ffn_setup()
    _L1_ffn_in = {k: v for k, v in _L1_ffn_all.items() if k in ('router_w', 'router_bias', 'Wu', 'Wg', 'Wd', 'Su', 'Sg', 'Sd')}
    del _L1_ffn_all
    return {'x': x, 'ctx_1024': ctx_1024, 'g_xattn': g_xattn, 'g_ffn': g_ffn, 'L0_xattn_in_proj_w': _L0_xattn_in['in_proj_w'], 'L0_xattn_conv_w': _L0_xattn_in['conv_w'], 'L0_xattn_conv_b': _L0_xattn_in['conv_b'], 'L0_xattn_x_proj_w': _L0_xattn_in['x_proj_w'], 'L0_xattn_dt_proj_w': _L0_xattn_in['dt_proj_w'], 'L0_xattn_dt_proj_b': _L0_xattn_in['dt_proj_b'], 'L0_xattn_A_log': _L0_xattn_in['A_log'], 'L0_xattn_D': _L0_xattn_in['D'], 'L0_ffn_gate_w': _L0_ffn_in['gate_w'], 'L0_ffn_cls_w': _L0_ffn_in['cls_w'], 'L0_ffn_extra_scale': _L0_ffn_in['extra_scale'], 'L0_ffn_extra_bias': _L0_ffn_in['extra_bias'], 'L0_ffn_wg': _L0_ffn_in['wg'], 'L0_ffn_wu': _L0_ffn_in['wu'], 'L0_ffn_wd': _L0_ffn_in['wd'], 'L0_ffn_sg': _L0_ffn_in['sg'], 'L0_ffn_su': _L0_ffn_in['su'], 'L0_ffn_sd': _L0_ffn_in['sd'], 'L1_xattn_in_proj_w': _L1_xattn_in['in_proj_w'], 'L1_xattn_conv_w': _L1_xattn_in['conv_w'], 'L1_xattn_conv_b': _L1_xattn_in['conv_b'], 'L1_xattn_x_proj_w': _L1_xattn_in['x_proj_w'], 'L1_xattn_dt_proj_w': _L1_xattn_in['dt_proj_w'], 'L1_xattn_dt_proj_b': _L1_xattn_in['dt_proj_b'], 'L1_xattn_A_log': _L1_xattn_in['A_log'], 'L1_xattn_D': _L1_xattn_in['D'], 'L1_ffn_router_w': _L1_ffn_in['router_w'], 'L1_ffn_router_bias': _L1_ffn_in['router_bias'], 'L1_ffn_Wu': _L1_ffn_in['Wu'], 'L1_ffn_Wg': _L1_ffn_in['Wg'], 'L1_ffn_Wd': _L1_ffn_in['Wd'], 'L1_ffn_Su': _L1_ffn_in['Su'], 'L1_ffn_Sg': _L1_ffn_in['Sg'], 'L1_ffn_Sd': _L1_ffn_in['Sd']}

def reference(x, ctx_1024, g_xattn, g_ffn, L0_xattn_in_proj_w, L0_xattn_conv_w, L0_xattn_conv_b, L0_xattn_x_proj_w, L0_xattn_dt_proj_w, L0_xattn_dt_proj_b, L0_xattn_A_log, L0_xattn_D, L0_ffn_gate_w, L0_ffn_cls_w, L0_ffn_extra_scale, L0_ffn_extra_bias, L0_ffn_wg, L0_ffn_wu, L0_ffn_wd, L0_ffn_sg, L0_ffn_su, L0_ffn_sd, L1_xattn_in_proj_w, L1_xattn_conv_w, L1_xattn_conv_b, L1_xattn_x_proj_w, L1_xattn_dt_proj_w, L1_xattn_dt_proj_b, L1_xattn_A_log, L1_xattn_D, L1_ffn_router_w, L1_ffn_router_bias, L1_ffn_Wu, L1_ffn_Wg, L1_ffn_Wd, L1_ffn_Su, L1_ffn_Sg, L1_ffn_Sd):
    import jax
    import jax.numpy as jnp

    def _L0_xattn_ref(hidden_states, z, in_proj_w, conv_w, conv_b, x_proj_w, dt_proj_w, dt_proj_b, A_log, D):
        import jax, jax.numpy as jnp
        import numpy as np
        import math
        B, L, DM = (2, 256, 128)
        DS, DC, EXP = (16, 4, 2)
        DI = EXP * DM
        DR = math.ceil(DM / 16)
        DT_MIN, DT_MAX, DT_FLOOR = (0.001, 0.1, 0.0001)

        def _ssm_forward(hidden_states, z, in_proj_w, conv_w, conv_b, x_proj_w, dt_proj_w, dt_proj_b, A_log, D):
            b = hidden_states.shape[0]
            x = jnp.einsum('ed,bld->bel', in_proj_w, hidden_states)
            xp = jnp.pad(x, ((0, 0), (0, 0), (DC - 1, 0)))
            xc = jax.lax.conv_general_dilated(xp, conv_w[:, None, :], window_strides=(1,), padding='VALID', dimension_numbers=('NCH', 'OIH', 'NCH'), feature_group_count=DI)
            u = jax.nn.silu(xc + conv_b[None, :, None])
            x_dbl = jnp.einsum('ke,bel->bkl', x_proj_w, u)
            dt_lo = x_dbl[:, :DR]
            Bm = x_dbl[:, DR:DR + DS]
            Cm = x_dbl[:, DR + DS:]
            delta = jax.nn.softplus(jnp.einsum('er,brl->bel', dt_proj_w, dt_lo) + dt_proj_b[None, :, None])
            A = -jnp.exp(A_log)

            def step(state, xs):
                d_t, B_t, C_t, u_t = xs
                dA = jnp.exp(d_t[..., None] * A)
                state = state * dA + (d_t * u_t)[..., None] * B_t[:, None, :]
                y_t = jnp.einsum('ben,bn->be', state, C_t)
                return (state, y_t)
            xs = (jnp.moveaxis(delta, -1, 0), jnp.moveaxis(Bm, -1, 0), jnp.moveaxis(Cm, -1, 0), jnp.moveaxis(u, -1, 0))
            state0 = jnp.zeros((b, DI, DS), delta.dtype)
            _, ys = jax.lax.scan(step, state0, xs)
            y = jnp.moveaxis(ys, 0, -1)
            y = y + D[None, :, None] * u
            y = y * jax.nn.silu(z)
            return jnp.swapaxes(y, 1, 2)
        return _ssm_forward(hidden_states, z, in_proj_w, conv_w, conv_b, x_proj_w, dt_proj_w, dt_proj_b, A_log, D)

    def _L0_ffn_ref(x, gate_w, cls_w, extra_scale, extra_bias, wg, wu, wd, sg, su, sd):
        import jax, jax.numpy as jnp
        import numpy as np
        TOPK = 2
        HID, INTER, E, SHARED_INTER = (256, 176, 14, 352)
        shape = x.shape
        d = shape[-1]
        xf = x.reshape(-1, d)
        T = xf.shape[0]
        n_exp = gate_w.shape[0]
        logits = xf @ cls_w.T * jax.nn.silu(xf @ gate_w.T)
        scores = jax.nn.softmax(jnp.abs(logits).astype(jnp.float32), axis=-1)
        biased = scores + extra_bias[None, :]
        _, idx = jax.lax.top_k(biased, TOPK)
        orig = 1.0 + scores * extra_scale[None, :]
        w = jnp.take_along_axis(orig, idx, axis=1).astype(x.dtype)
        combine = jnp.zeros((T, n_exp), x.dtype).at[jnp.arange(T)[:, None], idx].add(w)
        g = jax.nn.silu(jnp.einsum('td,efd->etf', xf, wg))
        u = jnp.einsum('td,efd->etf', xf, wu)
        o = jnp.einsum('etf,edf->etd', g * u, wd)
        y = jnp.einsum('etd,te->td', o, combine)
        z = jax.nn.silu(xf @ sg.T) * (xf @ su.T) @ sd.T
        return (y + z).reshape(shape)

    def _L1_xattn_ref(hidden_states, z, in_proj_w, conv_w, conv_b, x_proj_w, dt_proj_w, dt_proj_b, A_log, D):
        import jax, jax.numpy as jnp
        import numpy as np
        B_, L_, D_MODEL = (4, 256, 128)
        D_STATE, D_CONV, EXPAND = (16, 4, 2)
        D_INNER = EXPAND * D_MODEL
        DT_RANK = (D_MODEL + 15) // 16

        def silu(x):
            return x * jax.nn.sigmoid(x)
        Bsz, L, _ = hidden_states.shape
        d_inner, _, d_conv = conv_w.shape
        dt_rank = dt_proj_w.shape[1]
        d_state = A_log.shape[1]
        x = jnp.einsum('bld,ed->bel', hidden_states, in_proj_w)
        xc = jax.lax.conv_general_dilated(x, conv_w, window_strides=(1,), padding=[(d_conv - 1, 0)], feature_group_count=d_inner, dimension_numbers=('NCH', 'OIH', 'NCH'))
        x = silu(xc + conv_b[None, :, None])
        x_dbl = jnp.einsum('bdl,ed->bel', x, x_proj_w)
        dt_low, Bm, Cm = jnp.split(x_dbl, [dt_rank, dt_rank + d_state], axis=1)
        dt = jnp.einsum('brl,dr->bdl', dt_low, dt_proj_w)
        dt = jax.nn.softplus(dt + dt_proj_b[None, :, None])
        A = -jnp.exp(A_log)
        dt_t = jnp.moveaxis(dt, -1, 0)
        B_t = jnp.moveaxis(Bm, -1, 0)
        C_t = jnp.moveaxis(Cm, -1, 0)
        u_t = jnp.moveaxis(x, -1, 0)

        def step(state, inp):
            d, b, c, u = inp
            dA = jnp.exp(d[..., None] * A)
            state = state * dA + (d * u)[..., None] * b[:, None, :]
            y = jnp.einsum('bdn,bn->bd', state, c)
            return (state, y)
        state0 = jnp.zeros((Bsz, d_inner, d_state), x.dtype)
        _, ys = jax.lax.scan(step, state0, (dt_t, B_t, C_t, u_t))
        y = jnp.moveaxis(ys, 0, 2)
        y = y + D[None, :, None] * x
        y = y * silu(z)
        return jnp.swapaxes(y, 1, 2)

    def _L1_ffn_ref(x, router_w, router_bias, Wu, Wg, Wd, Su, Sg, Sd):
        import jax, jax.numpy as jnp
        import numpy as np
        DIM = 256
        EXPERT_DIM = 128
        N_EXPERTS = 16
        TOPK = 2
        N_SHARED = 1
        B, T = (4, 256)
        Bx, Tx, D = x.shape
        flat = x.reshape(Bx * Tx, D)
        logits = flat @ router_w.T
        scores = jax.nn.softmax(logits, axis=-1)
        _, topk_idx = jax.lax.top_k(logits + router_bias, TOPK)
        topk_scores = jnp.take_along_axis(scores, topk_idx, axis=-1)
        topk_scores = topk_scores / topk_scores.sum(-1, keepdims=True)
        combine = jnp.einsum('nk,nke->ne', topk_scores, jax.nn.one_hot(topk_idx, N_EXPERTS, dtype=scores.dtype))
        out = jnp.zeros_like(flat)
        for e in range(N_EXPERTS):
            h = jax.nn.silu(flat @ Wu[e]) * (flat @ Wg[e])
            out = out + combine[:, e:e + 1] * (h @ Wd[e])
        for s in range(N_SHARED):
            out = out + jax.nn.silu(flat @ Su[s]) * (flat @ Sg[s]) @ Sd[s]
        return out.reshape(Bx, Tx, D)
    x = x + jnp.tanh(g_xattn[0]) * _L0_xattn_ref(ctx_1024, _layernorm(x, axis=-1), L0_xattn_in_proj_w, L0_xattn_conv_w, L0_xattn_conv_b, L0_xattn_x_proj_w, L0_xattn_dt_proj_w, L0_xattn_dt_proj_b, L0_xattn_A_log, L0_xattn_D)
    x = x + jnp.tanh(g_ffn[0]) * _L0_ffn_ref(_layernorm(x, axis=-1), L0_ffn_gate_w, L0_ffn_cls_w, L0_ffn_extra_scale, L0_ffn_extra_bias, L0_ffn_wg, L0_ffn_wu, L0_ffn_wd, L0_ffn_sg, L0_ffn_su, L0_ffn_sd)
    x = x + jnp.tanh(g_xattn[1]) * _L1_xattn_ref(ctx_1024, _layernorm(x, axis=-1), L1_xattn_in_proj_w, L1_xattn_conv_w, L1_xattn_conv_b, L1_xattn_x_proj_w, L1_xattn_dt_proj_w, L1_xattn_dt_proj_b, L1_xattn_A_log, L1_xattn_D)
    x = x + jnp.tanh(g_ffn[1]) * _L1_ffn_ref(_layernorm(x, axis=-1), L1_ffn_router_w, L1_ffn_router_bias, L1_ffn_Wu, L1_ffn_Wg, L1_ffn_Wd, L1_ffn_Su, L1_ffn_Sg, L1_ffn_Sd)
    return x

_drawn_inputs = setup_inputs


def setup_inputs(seed=0):
    import zlib

    import numpy as np

    out = dict(_drawn_inputs(seed))
    spreads = {'g_ffn': (-1.0, 0.6),
     'L0_xattn_conv_b': (0.0, 0.1),
     'L0_xattn_D': (1.0, 0.2),
     'L1_xattn_D': (1.0, 0.6),
     'L1_ffn_router_bias': (0.0, 0.8)}
    factors = {'L0_xattn_dt_proj_w': 7.849,
     'L0_xattn_dt_proj_b': 3.278,
     'L0_xattn_A_log': 2.879,
     'L0_ffn_gate_w': 7.23,
     'L0_ffn_cls_w': 7.357,
     'L0_ffn_extra_scale': 8.0,
     'L0_ffn_extra_bias': 4.465,
     'L0_ffn_wg': 3.94,
     'L0_ffn_wu': 3.903,
     'L0_ffn_wd': 3.893,
     'L0_ffn_sg': 3.966,
     'L0_ffn_su': 3.918,
     'L0_ffn_sd': 3.91,
     'L1_xattn_in_proj_w': 4.705,
     'L1_xattn_conv_w': 4.817,
     'L1_xattn_conv_b': 8.0,
     'L1_xattn_x_proj_w': 8.0,
     'L1_xattn_dt_proj_w': 8.0,
     'L1_xattn_dt_proj_b': 8.0,
     'L1_xattn_A_log': 8.0,
     'L1_ffn_router_w': 8.0,
     'L1_ffn_Wu': 8.0,
     'L1_ffn_Wg': 8.0,
     'L1_ffn_Wd': 8.0,
     'L1_ffn_Su': 4.247,
     'L1_ffn_Sg': 4.185,
     'L1_ffn_Sd': 4.186}
    for name, (base, spread) in spreads.items():
        noise = np.random.default_rng([zlib.crc32(name.encode()), seed]).standard_normal(out[name].shape)
        drawn = base * np.exp(spread * noise) if base else spread * noise
        out[name] = jnp.asarray(drawn.astype(out[name].dtype))
    for name, factor in factors.items():
        out[name] = (out[name] * factor).astype(out[name].dtype)
    return out
```

```python
from contextlib import ExitStack

import concourse.bass as bass
from concourse import mybir
import numpy as np

F32 = mybir.dt.float32
BF16 = mybir.dt.bfloat16
U32 = mybir.dt.uint32
ALU = mybir.AluOpType
ACT = mybir.ActivationFunctionType
AX_X = mybir.AxisListType.X

P = 128
NB = 4
L = 256
D = 256
DCTX = 128
NH = D // P
NS = 16
DR = 8
TAPS = 4
NQ = NS // 2
GRP = 32
EXPERTS = (14, 16)
INTER = (176, 128)
SHARED = (352, 256)
PIECE = 256
HIDDEN = tuple(EXPERTS[y] * INTER[y] + SHARED[y] for y in range(2))
NP = tuple(HIDDEN[y] // PIECE for y in range(2))
WCOLS = NH * 2 * PIECE + 2 * D
EPS = 1e-5
DU = 3
SMALL = 16 * 10

PK, at = {}, 0
for _name, _n in (("conv_b", NH), ("dt_b", NH), ("D", NH), ("A_log", NH * NS), ("xp", NH * 3 * GRP),
                  ("xc", NH * NS), ("w_in", D), ("w_dt", D)):
    PK[_name] = (at, at + _n)
    at += _n
PKCOLS = at
RW = (2 * EXPERTS[0], EXPERTS[1])


def pieces_before(m, y):
    return NP[0] * m if y == 0 else NP[1] * m + NB * (NP[0] - NP[1])


def segments(y, j):
    out, f = [], j * PIECE
    while f < (j + 1) * PIECE:
        e = min(f // INTER[y], EXPERTS[y])
        end = (j + 1) * PIECE if e == EXPERTS[y] else min((e + 1) * INTER[y], (j + 1) * PIECE)
        out.append((f - j * PIECE, end - j * PIECE, e))
        f = end
    return out


def wait(eng, sem, value):
    if not isinstance(value, int) or value > 0:
        eng.wait_ge(sem, value)


def build(nc, x_in, ctx_in, pack_in, convw_in, gates_in, weights_in, router_in, rows_in, const_in, sel_in, out):
    with ExitStack() as stack:
        def sb(name, shape, dt=F32):
            return stack.enter_context(nc.sbuf_tensor(name, shape, dt))

        def ps(name, shape):
            return stack.enter_context(nc.psum_tensor(name, shape, F32))

        def sem(name):
            return stack.enter_context(nc.semaphore(name))

        x = sb("x", [P, NB, NH, D])
        weights = sb("weights", [P, NP[0], WCOLS])
        ident = sb("ident", [P, P])
        iota = sb("iota", [P, NS])
        sel = sb("sel", [3 * GRP, NS, P], BF16)
        ctx_t = sb("ctx_t", [P, NB, L + TAPS - 1])
        pack = [sb(f"pack{y}", [P, PKCOLS]) for y in range(2)]
        router_w = [sb(f"router_w{y}", [P, NH, RW[y]]) for y in range(2)]
        rows = sb("rows", [P, 2 * EXPERTS[0] + EXPERTS[1]])
        gates = sb("gates", [P, 4])
        gate_f = sb("gate_f", [P, 4])
        a_neg = sb("a_neg", [P, 2, NH, NS])
        minus_half = sb("minus_half", [P, NH])
        ones = sb("ones", [P, 1])
        eps = sb("eps", [P, NH])
        pause = sb("pause", [P, 1])
        u = [sb(f"u{y}", [P, NH, NB, L]) for y in range(2)]
        delta = [sb(f"delta{y}", [P, NH, NB, L]) for y in range(2)]
        bstack = [sb(f"bstack{y}", [3 * GRP, NB, L], BF16) for y in range(2)]
        c_tok = [sb(f"c_tok{y}", [P, NB, NH, NS]) for y in range(2)]
        convw = sb("convw", [P, TAPS, D])
        w_taps = sb("w_taps", [P, TAPS, D])
        xdbl = sb("xdbl", [3 * GRP, NB, L])
        rest = sb("rest", [3 * GRP, 2 * L])
        mid = sb("mid", [3 * GRP, 2 * L], BF16)
        s1 = sb("s1", [P, NH * NB * L])
        du = sb("du", [P, NH, L])
        delta_now = sb("delta_now", [P, NH, L])
        skip = sb("skip", [P, NH, L])
        c_now = sb("c_now", [P, NH, NS])
        decay = sb("decay", [P, 2, NH * 2 * L])
        state = sb("state", [P, 2, NH * 2 * L])
        acc = sb("acc", [P, NH, D])
        z_stat = sb("z_stat", [P, NH, 6])
        z_mv = sb("z_mv", [P, NH, 2])
        z_rstd = sb("z_rstd", [P, NH])
        zn = sb("zn", [P, NH, L])
        z_th = sb("z_th", [P, NH, L])
        z_silu = sb("z_silu", [P, NH, L])
        gated = sb("gated", [P, NH, D])
        x_stat = sb("x_stat", [P, NH, 6])
        x_mv = sb("x_mv", [P, NH, 2])
        x_rstd = sb("x_rstd", [P, NH])
        xn = sb("xn", [P, NH, D])
        xn_t = sb("xn_t", [P, NH, L])
        cw = [sb(f"cw{y}", [P, NH, EXPERTS[y] + 1]) for y in range(2)]
        lg = sb("lg", [P, NH, 32])
        r_a = sb("r_a", [P, NH, NS])
        r_b = sb("r_b", [P, NH, NS])
        r_e = sb("r_e", [P, NH, NS])
        r_one = sb("r_one", [P, NH])
        r_sum = sb("r_sum", [P, NH])
        top = sb("top", [P, NH, 8])
        top_i = sb("top_i", [P, NH, 8], U32)
        top_f = sb("top_f", [P, NH, 8])
        mask = sb("mask", [P, NH, NS])
        th = sb("th", [P, NH, PIECE])
        silu = sb("silu", [P, NH, PIECE])
        hid = sb("hid", [P, NH, PIECE])
        hid_t = sb("hid_t", [P, 2, 2, NH, P])

        ps_gu = ps("ps_gu", [P, NH, 512])
        ps_t = ps("ps_t", [P, 512])
        ps_out = ps("ps_out", [P, 512])
        ps_br = ps("ps_br", [P, 2, 512])
        ps_ht = ps("ps_ht", [P, 2, 512])

        small_in = sem("small_in")
        convw_in_s = [sem(f"convw_in{y}") for y in range(2)]
        x_loaded = sem("x_loaded")
        piece_in = [sem(f"piece_in{j}") for j in range(NP[0])]
        stored = sem("stored")
        const_set = sem("const_set")
        gate_tanh = sem("gate_tanh")
        gate_ready = sem("gate_ready")
        edge_set = sem("edge_set")
        a_exp = sem("a_exp")
        a_ready = sem("a_ready")
        taps_ready = sem("taps_ready")
        conv_psum = sem("conv_psum")
        u_ready = sem("u_ready")
        xdbl_psum = sem("xdbl_psum")
        xdbl_ready = sem("xdbl_ready")
        hi_ready = sem("hi_ready")
        split_step = sem("split_step")
        dt_psum = sem("dt_psum")
        abs_done = sem("abs_done")
        relu_done = sem("relu_done")
        exp_done = sem("exp_done")
        ln_done = sem("ln_done")
        softplus_step = sem("softplus_step")
        c_psum = sem("c_psum")
        c_ready = sem("c_ready")
        du_ready = sem("du_ready")
        skip_ready = sem("skip_ready")
        skip_psum = sem("skip_psum")
        acc_init = sem("acc_init")
        brep_psum = sem("brep_psum")
        dbu_done = sem("dbu_done")
        decay_ready = sem("decay_ready")
        scan_done = sem("scan_done")
        state_psum = sem("state_psum")
        acc_done = sem("acc_done")
        z_stat_done = sem("z_stat_done")
        z_mv_done = sem("z_mv_done")
        z_eps_done = sem("z_eps_done")
        z_rstd_done = sem("z_rstd_done")
        zn_done = sem("zn_done")
        z_tanh = sem("z_tanh")
        z_silu_done = sem("z_silu_done")
        z_psum = sem("z_psum")
        gated_done = sem("gated_done")
        x_gated = sem("x_gated")
        x_stat_done = sem("x_stat_done")
        x_mv_done = sem("x_mv_done")
        x_eps_done = sem("x_eps_done")
        x_rstd_done = sem("x_rstd_done")
        xn_done = sem("xn_done")
        xn_psum = sem("xn_psum")
        xn_t_ready = sem("xn_t_ready")
        logits_psum = sem("logits_psum")
        logits_done = sem("logits_done")
        router_act = sem("router_act")
        router_exp_in = sem("router_exp_in")
        router_exp = sem("router_exp")
        router_step = sem("router_step")
        gu_psum = sem("gu_psum")
        tanh_done = sem("tanh_done")
        silu_done = sem("silu_done")
        hid_done = sem("hid_done")
        hid_psum = sem("hid_psum")
        hid_t_ready = sem("hid_t_ready")
        down_done = sem("down_done")
        x_added = sem("x_added")

        def pk(y, name):
            a, b = PK[name]
            return pack[y][:, a:b]

        def xp(y, h):
            return pk(y, "xp")[:, h * 3 * GRP:(h + 1) * 3 * GRP]

        def wide(y, j, d):
            return weights[:, j, d * 2 * PIECE:(d + 1) * 2 * PIECE]

        def down(j, blk):
            a = NH * 2 * PIECE + blk * D
            return weights[:, j, a:a + D]

        block = stack.enter_context(nc.Block())

        def stages(eng, stage):
            stage(0, None, 0)
            stage(1, 0, 0)
            with eng.Fori(2, NB) as k:
                stage(k, 0, 0)
            stage(NB, 0, 1)
            with eng.Fori(NB + 1, 2 * NB) as k:
                stage(k, 1, 1)
            stage(2 * NB, 1, None)

        def slots(my):
            return max(NP[my], NQ + 1) if my is not None else NQ + 1

        @block.sync
        def _(sp):
            sp.dma_start(ctx_t[:], ctx_in).then_inc(small_in, 16)
            for y in range(2):
                sp.dma_start(pack[y][:], pack_in[y]).then_inc(small_in, 16)
            sp.dma_start(convw[:], convw_in[0:1, :].broadcast_to([P, TAPS * D]).rearrange(
                "p (k e) -> p k e", k=TAPS)).then_inc(convw_in_s[0], 16)
            sp.dma_start(sel[:], sel_in).then_inc(small_in, 16)
            sp.dma_start(ident[:], const_in[:, 0:P]).then_inc(small_in, 16)
            sp.dma_start(iota[:], const_in[:, P:P + NS]).then_inc(small_in, 16)
            sp.dma_start(gates[:], gates_in.broadcast_to([P, 4])).then_inc(small_in, 16)
            for y in range(2):
                sp.dma_start(router_w[y][:], router_in[y]).then_inc(small_in, 16)
            sp.dma_start(rows[:], rows_in.broadcast_to([P, 2 * EXPERTS[0] + EXPERTS[1]])).then_inc(small_in, 16)
            sp.dma_start(x[:], x_in).then_inc(x_loaded, 16)
            for j in range(NP[0]):
                sp.dma_start(weights[:, j, :], weights_in[0][j]).then_inc(piece_in[j], 16)
            sp.wait_ge(taps_ready, 1)
            sp.dma_start(convw[:], convw_in[1:2, :].broadcast_to([P, TAPS * D]).rearrange(
                "p (k e) -> p k e", k=TAPS)).then_inc(convw_in_s[1], 16)
            for j in range(NP[1]):
                sp.wait_ge(down_done, pieces_before(NB - 1, 0) + j + 1)
                sp.dma_start(weights[:, j, :], weights_in[1][j]).then_inc(piece_in[j], 16)
            for b in range(NB):
                sp.wait_ge(x_added, NB + b + 1)
                sp.dma_start(out[b], x[:, b]).then_inc(stored, 16)
            sp.wait_ge(stored, 16 * NB)

        @block.gpsimd
        def _(pool):
            nc.gpsimd.memset(minus_half[:], -0.5).then_inc(const_set, 1)
            nc.gpsimd.memset(ones[:], 1.0).then_inc(const_set, 1)
            nc.gpsimd.memset(eps[:], EPS).then_inc(const_set, 1)
            for y in range(2):
                nc.gpsimd.memset(cw[y][:, :, EXPERTS[y]:EXPERTS[y] + 1], 0.5).then_inc(const_set, 1)
            pool.wait_ge(const_set, 5)
            pool.wait_ge(small_in, SMALL)

            def rstd(var, to, ready, eps_done, done, count):
                pool.wait_ge(ready, NH * (count + 1))
                nc.gpsimd.tensor_tensor(to, var, eps[:], ALU.add).then_inc(eps_done, 1)
                pool.wait_ge(eps_done, count + 1)
                nc.gpsimd.tensor_tensor(to, to, minus_half[:], ALU.pow).then_inc(done, 1)

            def stage(k, my, sy):
                if sy is None:
                    return
                rstd(z_mv[:, :, 1], z_rstd[:], z_mv_done, z_eps_done, z_rstd_done, k)
                rstd(x_mv[:, :, 1], x_rstd[:], x_mv_done, x_eps_done, x_rstd_done, k)

            stages(pool, stage)

        @block.scalar
        def _(act):
            act.wait_ge(small_in, SMALL)
            nc.scalar.activation(gate_f[:], gates[:], ACT.Tanh).then_inc(gate_tanh, 1)
            for y in range(2):
                nc.scalar.activation(a_neg[:, y].rearrange("p h n -> p (h n)"), pk(y, "A_log"),
                                     ACT.Exp).then_inc(a_exp, 1)

            def prep(y):
                for tb in range(2):
                    for h in range(NH):
                        act.wait_ge(conv_psum, 4 * y + 2 * tb + h + 1)
                        nc.scalar.activation(u[y][:, h, 2 * tb:2 * tb + 2].rearrange("p b l -> p (b l)"),
                                             ps_gu[:, h], ACT.Silu,
                                             bias=pk(y, "conv_b")[:, h:h + 1]).then_inc(u_ready, 1)
                for tb in range(2):
                    xd = xdbl[:, 2 * tb:2 * tb + 2].rearrange("p b l -> p (b l)")
                    act.wait_ge(xdbl_psum, 2 * y + tb + 1)
                    if y:
                        act.wait_ge(dt_psum, 4)
                        act.wait_ge(split_step, 8)
                    nc.scalar.activation(xd, ps_br[0:3 * GRP, tb], ACT.Identity).then_inc(xdbl_ready, 1)
                    nc.scalar.activation(bstack[y][:, 2 * tb:2 * tb + 2].rearrange("p b l -> p (b l)"),
                                         ps_br[0:3 * GRP, tb], ACT.Identity).then_inc(hi_ready, 1)
                act.wait_ge(c_psum, y + 1)
                nc.scalar.activation(c_tok[y][:].rearrange("p b t n -> p (b t n)"), ps_out[:, 0:8 * NS],
                                     ACT.Identity).then_inc(c_ready, 1)
                w = decay[:].rearrange("p s f -> p (s f)")
                lnw = state[:].rearrange("p s f -> p (s f)")
                wait(act, softplus_step, 4 * y)
                for i in range(4):
                    act.wait_ge(dt_psum, 4 * y + i + 1)
                    nc.scalar.activation(w[:, i * 512:(i + 1) * 512], ps_ht[:, i % 2], ACT.Abs,
                                         bias=pk(y, "dt_b")[:, i % 2:i % 2 + 1]).then_inc(abs_done, 1)
                act.wait_ge(abs_done, 4 * y + 4)
                nc.scalar.activation(w, w, ACT.Exp, scale=-1.0).then_inc(exp_done, 1)
                act.wait_ge(exp_done, y + 1)
                act.wait_ge(const_set, 5)
                nc.scalar.activation(lnw, w, ACT.Ln, bias=ones[:, 0:1]).then_inc(ln_done, 1)

            prep(0)
            prep(1)

            def decays(k, sy, b, q):
                if q == 0:
                    act.wait_ge(a_ready, 1)
                    act.wait_ge(edge_set, 1)
                    act.wait_ge(du_ready, DU * k + 1)
                wait(act, scan_done, NQ * k + q - 1)
                for h in range(NH):
                    for i in range(2):
                        o = (h * 2 + i) * L
                        ins = nc.scalar.activation(decay[:, q % 2, o + 1:o + L], delta_now[:, h, 1:L],
                                                   ACT.Exp, scale=a_neg[:, sy, h, 2 * q + i:2 * q + i + 1])
                ins.then_inc(decay_ready, 1)

            def stage(k, my, sy):
                m = k - 1
                if my is not None:
                    base = pieces_before(m, my)
                    if my == 0:
                        act.wait_ge(logits_done, m + 1)
                        nc.scalar.activation(r_b[:, :, 0:EXPERTS[0]], lg[:, :, EXPERTS[0]:2 * EXPERTS[0]],
                                             ACT.Tanh, scale=0.5).then_inc(router_act, 1)
                    act.wait_ge(router_exp_in, m + 1)
                    nc.scalar.activation(r_e[:, :, 0:EXPERTS[my]], r_a[:, :, 0:EXPERTS[my]],
                                         ACT.Exp).then_inc(router_exp, 1)

                def tanh(j, t):
                    act.wait_ge(gu_psum, 2 * (base + j) + t + 1)
                    wait(act, silu_done, 2 * base + (2 * (j - 1) + t + 1 if j else 0))
                    nc.scalar.activation(th[:, t], ps_gu[:, t, 0:PIECE], ACT.Tanh,
                                         scale=0.5).then_inc(tanh_done, 1)

                def turn(j):
                    act.wait_ge(hid_psum, base + j + 1)
                    wait(act, down_done, base + (j - 1 if j >= 2 else 0))
                    nc.scalar.activation(hid_t[:, j % 2].rearrange("p k t n -> p (k t n)"), ps_t[:],
                                         ACT.Identity).then_inc(hid_t_ready, 1)

                for j in range(slots(my) + 1):
                    if my is not None and j < NP[my]:
                        tanh(j, 0)
                    if my is not None and 1 <= j <= NP[my]:
                        turn(j - 1)
                    if my is not None and j < NP[my]:
                        tanh(j, 1)
                    if sy is None:
                        continue
                    b = k - NB * sy
                    if j == 0:
                        decays(k, sy, b, 0)
                        act.wait_ge(skip_psum, k + 1)
                        wait(act, gated_done, k)
                        nc.scalar.activation(acc[:].rearrange("p t e -> p (t e)"), ps_ht[:, 1],
                                             ACT.Identity).then_inc(acc_init, 1)
                    if j + 1 < NQ:
                        decays(k, sy, b, j + 1)
                    if j == 4:
                        act.wait_ge(zn_done, 2 * k + 2)
                        nc.scalar.activation(z_th[:], zn[:], ACT.Tanh, scale=0.5).then_inc(z_tanh, 1)
                if sy is not None:
                    act.wait_ge(xn_psum, k + 1)
                    if my is not None:
                        act.wait_ge(gu_psum, 2 * (base + NP[my]))
                    nc.scalar.activation(xn_t[:].rearrange("p d t -> p (d t)"), ps_ht[:, 1],
                                         ACT.Identity).then_inc(xn_t_ready, 1)

            stages(act, stage)

        @block.tensor
        def _(pe):
            pe.wait_ge(small_in, SMALL)

            def prep(y):
                pe.wait_ge(taps_ready, y + 1)
                for tb in range(2):
                    for h in range(NH):
                        i = 4 * y + 2 * tb + h
                        wait(pe, u_ready, i - 1)
                        for k in range(TAPS):
                            mm = pe.matmul(ps_gu[:, h], w_taps[:, k, h * P:(h + 1) * P],
                                           ctx_t[:, 2 * tb:2 * tb + 2, k:k + L],
                                           start=(k == 0), stop=(k == TAPS - 1))
                        mm.then_inc(conv_psum, 1)
                if y:
                    pe.wait_ge(hi_ready, 2)
                for tb in range(2):
                    pe.wait_ge(u_ready, 4 * y + 2 * tb + 2)
                    for h in range(NH):
                        mm = pe.matmul(ps_br[0:3 * GRP, tb], xp(y, h),
                                       u[y][:, h, 2 * tb:2 * tb + 2].rearrange("p b l -> p (b l)"),
                                       start=(h == 0), stop=(h == 1))
                    mm.then_inc(xdbl_psum, 1)
                wait(pe, c_ready, y)
                for t in range(2 * NB):
                    for h in range(NH):
                        mm = pe.matmul(ps_out[:, t * NS:(t + 1) * NS],
                                       u[y][:, h, t // 2, (t % 2) * P:(t % 2 + 1) * P],
                                       pk(y, "xc")[:, h * NS:(h + 1) * NS], start=(h == 0), stop=(h == 1))
                mm.then_inc(c_psum, 1)
                for i in range(4):
                    tb, h = i // 2, i % 2
                    pe.wait_ge(xdbl_ready, 2 * y + tb + 1)
                    wait(pe, abs_done, 4 * y + i - 1)
                    wait(pe, relu_done, 4 * y + i - 1)
                    pe.matmul(ps_ht[:, h], pk(y, "w_dt")[0:GRP, h * P:(h + 1) * P],
                              xdbl[0:GRP, 2 * tb:2 * tb + 2].rearrange("p b l -> p (b l)"),
                              start=True, stop=True).then_inc(dt_psum, 1)

            prep(0)
            prep(1)
            pe.wait_ge(abs_done, 8)
            pe.wait_ge(relu_done, 8)
            pe.wait_ge(c_ready, 2)

            def brep(k, sy, b, q):
                pe.wait_ge(split_step, 8 * (sy + 1))
                wait(pe, dbu_done, NQ * k + q - 1)
                for i in range(2):
                    mm = pe.matmul(ps_br[:, q % 2, i * L:(i + 1) * L], sel[:, 2 * q + i, :],
                                   bstack[sy][:, b, :], start=True, stop=True)
                mm.then_inc(brep_psum, 1)

            def turn_states(k, q):
                pe.wait_ge(scan_done, NQ * k + q + 1)
                for i in range(2):
                    n = 2 * q + i
                    wait(pe, acc_done, 2 * NS * k + 2 * (n - 1) if n >= 2 else 0)
                    if n == 0:
                        wait(pe, gated_done, k)
                    if n == 1:
                        pe.wait_ge(acc_init, k + 1)
                    for t in range(NH):
                        for h in range(NH):
                            o = (h * 2 + i) * L + t * P
                            mm = pe.transpose(ps_ht[:, i, t * D + h * P:t * D + (h + 1) * P],
                                              state[:, q % 2, o:o + P], ident[:])
                    mm.then_inc(state_psum, 1)

            def turn4(bank, src, done):
                for t in range(NH):
                    for h in range(NH):
                        mm = pe.transpose(bank[:, t * D + h * P:t * D + (h + 1) * P],
                                          src[:, h, t * P:(t + 1) * P], ident[:])
                mm.then_inc(done, 1)

            def stage(k, my, sy):
                m = k - 1
                if my is not None:
                    base = pieces_before(m, my)
                    pe.wait_ge(xn_t_ready, m + 1)
                    wait(pe, hid_t_ready, base)
                    for t in range(NH):
                        for d in range(NH):
                            mm = pe.matmul(ps_t[:, t * 32:t * 32 + RW[my]], xn_t[:, d, t * P:(t + 1) * P],
                                           router_w[my][:, d], start=(d == 0), stop=(d == 1))
                    mm.then_inc(logits_psum, 1)

                def gate_up(j, t):
                    if j == 0 and t == 0:
                        wait(pe, hid_done, 2 * base)
                    elif j >= 1:
                        pe.wait_ge(hid_done, 2 * (base + j - 1) + t + 1)
                    if t == 0:
                        pe.wait_ge(piece_in[j], 16 * (my + 1))
                    for d in range(NH):
                        mm = pe.matmul(ps_gu[:, t], xn_t[:, d, t * P:(t + 1) * P], wide(my, j, d),
                                       start=(d == 0), stop=(d == 1))
                    mm.then_inc(gu_psum, 1)

                def turn(j):
                    pe.wait_ge(hid_done, 2 * (base + j) + 2)
                    wait(pe, hid_t_ready, base + j)
                    for blk in range(2):
                        for t in range(NH):
                            o = (blk * 2 + t) * P
                            mm = pe.transpose(ps_t[:, o:o + P], hid[:, t, blk * P:(blk + 1) * P], ident[:])
                    mm.then_inc(hid_psum, 1)

                def down_product(j):
                    pe.wait_ge(hid_t_ready, base + j + 1)
                    if j == 0:
                        wait(pe, x_added, m)
                    for t in range(NH):
                        for blk in range(2):
                            mm = pe.matmul(ps_out[:, t * D:(t + 1) * D], hid_t[:, j % 2, blk, t],
                                           down(j, blk), start=(j == 0 and blk == 0 and t == 0),
                                           stop=(j == NP[my] - 1 and blk == 1 and t == 1),
                                           skip_group_check=True)
                    mm.then_inc(down_done, 1)

                for j in range(slots(my) + 1):
                    on = my is not None
                    if on and j < NP[my]:
                        gate_up(j, 0)
                    if on and 1 <= j <= NP[my]:
                        turn(j - 1)
                    if on and j < NP[my]:
                        gate_up(j, 1)
                    if sy is not None:
                        b = k - NB * sy
                        if j == 0:
                            pe.wait_ge(skip_ready, NH * (k + 1))
                            wait(pe, xn_t_ready, k)
                            turn4(ps_ht[:, 1], skip, skip_psum)
                            brep(k, sy, b, 0)
                            brep(k, sy, b, 1)
                        if 1 <= j <= NQ:
                            turn_states(k, j - 1)
                            if j + 1 < NQ:
                                brep(k, sy, b, j + 1)
                        if j == slots(my):
                            pe.wait_ge(z_silu_done, k + 1)
                            pe.wait_ge(acc_done, 2 * NS * k + 2 * NS - 2)
                            turn4(ps_ht[:, 0], z_silu, z_psum)
                            pe.wait_ge(xn_done, NH * (k + 1))
                            pe.wait_ge(acc_done, 2 * NS * (k + 1))
                            turn4(ps_ht[:, 1], xn, xn_psum)
                    if on and 1 <= j <= NP[my]:
                        down_product(j - 1)

            stages(pe, stage)

        @block.vector
        def _(dve):
            dve.wait_ge(small_in, SMALL)
            dve.wait_ge(const_set, 5)
            dve.wait_ge(gate_tanh, 1)
            nc.vector.tensor_scalar(gate_f[:, 0:2], gate_f[:, 0:2], 0.5, None, ALU.mult).then_inc(gate_ready, 1)
            dve.wait_ge(a_exp, 2)
            nc.vector.tensor_scalar(a_neg[:], a_neg[:], -1.0, None, ALU.mult).then_inc(a_ready, 1)

            def prep(y):
                dve.wait_ge(convw_in_s[y], 16)
                wait(dve, conv_psum, 4 * y)
                nc.vector.tensor_tensor(w_taps[:], pk(y, "w_in").unsqueeze(1).broadcast_to([P, TAPS, D]),
                                        convw[:], ALU.mult).then_inc(taps_ready, 1)
                for tb in range(2):
                    n = 8 * y + 4 * tb
                    xd = xdbl[:, 2 * tb:2 * tb + 2].rearrange("p b l -> p (b l)")
                    bs = bstack[y][:, 2 * tb:2 * tb + 2].rearrange("p b l -> p (b l)")
                    dve.wait_ge(hi_ready, 2 * y + tb + 1)
                    dve.wait_ge(xdbl_ready, 2 * y + tb + 1)
                    nc.vector.tensor_tensor(rest[:], xd, bs, ALU.subtract).then_inc(split_step, 1)
                    dve.wait_ge(split_step, n + 1)
                    nc.vector.tensor_copy(mid[:], rest[:]).then_inc(split_step, 1)
                    dve.wait_ge(split_step, n + 2)
                    nc.vector.tensor_copy(bs[GRP:2 * GRP], mid[GRP:2 * GRP]).then_inc(split_step, 1)
                    nc.vector.tensor_tensor(bs[2 * GRP:3 * GRP], rest[2 * GRP:3 * GRP], mid[2 * GRP:3 * GRP],
                                            ALU.subtract).then_inc(split_step, 1)
                    dve.wait_ge(split_step, n + 4)
                for i in range(4):
                    tb, h = i // 2, i % 2
                    dve.wait_ge(abs_done, 4 * y + i + 1)
                    nc.vector.tensor_scalar(delta[y][:, h, 2 * tb:2 * tb + 2].rearrange("p b l -> p (b l)"),
                                            ps_ht[:, h], pk(y, "dt_b")[:, h:h + 1], 0.0,
                                            ALU.add, ALU.max).then_inc(relu_done, 1)
                w = decay[:].rearrange("p s f -> p (s f)")
                lnw = state[:].rearrange("p s f -> p (s f)")
                dve.wait_ge(exp_done, y + 1)
                nc.vector.tensor_scalar(s1[:], w, 1.0, -1.0, ALU.add, ALU.add).then_inc(softplus_step, 1)
                dve.wait_ge(softplus_step, 4 * y + 1)
                nc.vector.tensor_tensor(s1[:], w, s1[:], ALU.subtract).then_inc(softplus_step, 1)
                dve.wait_ge(softplus_step, 4 * y + 2)
                dve.wait_ge(ln_done, y + 1)
                nc.vector.tensor_tensor(s1[:], lnw, s1[:], ALU.add).then_inc(softplus_step, 1)
                dve.wait_ge(softplus_step, 4 * y + 3)
                dve.wait_ge(relu_done, 4 * y + 4)
                nc.vector.tensor_tensor(
                    delta[y][:].rearrange("p h (a c) l -> p a h (c l)", a=2),
                    delta[y][:].rearrange("p h (a c) l -> p a h (c l)", a=2),
                    s1[:].rearrange("p (a h f) -> p a h f", a=2, h=NH), ALU.add).then_inc(softplus_step, 1)

            prep(0)
            prep(1)
            dve.wait_ge(softplus_step, 8)
            nc.vector.memset(decay[:].rearrange("p s (g l) -> p (s g) l", l=L)[:, :, 0:1], 0.0).then_inc(edge_set, 1)

            def hold():
                nc.vector.memset(pause[:], 0.0)

            def norm(src, stat, mv, rstd, to, stat_done, mv_done, rstd_done, done, k):
                def stats():
                    for t in range(NH):
                        nc.vector.bn_stats(stat[:, t], src(t)).then_inc(stat_done, 1)

                def means():
                    dve.wait_ge(stat_done, NH * (k + 1))
                    hold()
                    for t in range(NH):
                        nc.vector.bn_aggr(mv[:, t], stat[:, t]).then_inc(mv_done, 1)

                def scaled():
                    dve.wait_ge(mv_done, NH * (k + 1))
                    dve.wait_ge(rstd_done, k + 1)
                    for t in range(NH):
                        nc.vector.tensor_scalar(to[:, t], src(t), mv[:, t, 0:1], rstd[:, t:t + 1],
                                                ALU.subtract, ALU.mult).then_inc(done, 1)
                return stats, means, scaled

            def router(m, my):
                ne = EXPERTS[my]
                base = 16 * m

                step = [0]

                def chain(ins):
                    step[0] += 1
                    ins.then_inc(router_step, 1)
                    dve.wait_ge(router_step, base + step[0])

                def over(a):
                    return a.unsqueeze(2).broadcast_to([P, NH, ne])

                a, e, bt = r_a[:, :, 0:ne], r_e[:, :, 0:ne], r_b[:, :, 0:ne]
                dve.wait_ge(logits_psum, m + 1)
                src = ps_t[:, 0:64].rearrange("p (t n) -> p t n", t=NH)[:, :, 0:RW[my]]
                nc.vector.tensor_copy(lg[:, :, 0:RW[my]], src).then_inc(logits_done, 1)
                dve.wait_ge(logits_done, m + 1)
                if my == 0:
                    dve.wait_ge(router_act, m + 1)
                    chain(nc.vector.scalar_tensor_tensor(out=bt, in0=bt, scalar=1.0, in1=lg[:, :, ne:2 * ne],
                                                         op0=ALU.add, op1=ALU.mult))
                    chain(nc.vector.scalar_tensor_tensor(out=bt, in0=bt, scalar=0.5, in1=lg[:, :, 0:ne],
                                                         op0=ALU.mult, op1=ALU.mult))
                    chain(nc.vector.scalar_tensor_tensor(out=bt, in0=bt, scalar=-1.0, in1=bt,
                                                         op0=ALU.mult, op1=ALU.max))
                else:
                    bt = lg[:, :, 0:ne]
                chain(nc.vector.tensor_reduce(r_one[:], bt, AX_X, ALU.max))
                nc.vector.tensor_tensor(a, bt, over(r_one[:]), ALU.subtract).then_inc(router_exp_in, 1)
                dve.wait_ge(router_exp, m + 1)
                if my == 0:
                    chain(nc.vector.tensor_reduce(r_sum[:], e, AX_X, ALU.add))
                    chain(nc.vector.reciprocal(r_sum[:], r_sum[:]))
                    chain(nc.vector.tensor_tensor(e, e, over(r_sum[:]), ALU.mult))
                    bias = rows[:, ne:2 * ne]
                    ranked = e
                else:
                    bias = rows[:, 2 * EXPERTS[0]:]
                    ranked = bt
                chain(nc.vector.tensor_tensor(a, ranked, bias.unsqueeze(1).broadcast_to([P, NH, ne]), ALU.add))
                hold()
                for t in range(NH):
                    ins = nc.vector.max(top[:, t], r_a[:, t, 0:ne])
                chain(ins)
                hold()
                for t in range(NH):
                    ins = nc.vector.max_index(top_i[:, t], top[:, t], r_a[:, t, 0:ne])
                chain(ins)
                chain(nc.vector.tensor_copy(top_f[:], top_i[:]))
                for t in range(NH):
                    ins = nc.vector.tensor_scalar(mask[:, t, 0:ne], iota[:, 0:ne], top_f[:, t, 0:1], 0.5,
                                                  ALU.is_equal, ALU.mult)
                    ins2 = nc.vector.tensor_scalar(r_a[:, t, 0:ne], iota[:, 0:ne], top_f[:, t, 1:2], 0.5,
                                                   ALU.is_equal, ALU.mult)
                chain(ins2)
                mk = mask[:, :, 0:ne]
                chain(nc.vector.tensor_tensor(mk, mk, a, ALU.add))
                if my == 0:
                    chain(nc.vector.tensor_tensor(e, e, rows[:, 0:ne].unsqueeze(1).broadcast_to([P, NH, ne]),
                                                  ALU.mult))
                    chain(nc.vector.scalar_tensor_tensor(out=cw[0][:, :, 0:ne], in0=e, scalar=1.0, in1=mk,
                                                         op0=ALU.add, op1=ALU.mult))
                else:
                    chain(nc.vector.tensor_tensor(e, e, mk, ALU.mult))
                    chain(nc.vector.tensor_reduce(r_sum[:], e, AX_X, ALU.add))
                    chain(nc.vector.reciprocal(r_sum[:], r_sum[:]))
                    chain(nc.vector.scalar_tensor_tensor(out=cw[1][:, :, 0:ne], in0=e, scalar=0.5,
                                                         in1=over(r_sum[:]), op0=ALU.mult, op1=ALU.mult))
                dve.sem_inc(router_step, 16 - step[0])

            def stage(k, my, sy):
                m = k - 1
                on, son = my is not None, sy is not None
                if on:
                    base = pieces_before(m, my)
                    router(m, my)
                if son:
                    b = k - NB * sy
                    bank = slice(0, 512)
                    z_norm = norm(lambda t: x[:, b, t], z_stat, z_mv, z_rstd, zn, z_stat_done, z_mv_done,
                                  z_rstd_done, zn_done, k)
                    x_norm = norm(lambda t: x[:, b, t], x_stat, x_mv, x_rstd, xn, x_stat_done, x_mv_done,
                                  x_rstd_done, xn_done, k)
                    nc.vector.tensor_copy(delta_now[:], delta[sy][:, :, b]).then_inc(du_ready, 1)
                    nc.vector.tensor_tensor(du[:], delta[sy][:, :, b], u[sy][:, :, b], ALU.mult).then_inc(du_ready, 1)
                    wait(dve, skip_psum, k)
                    for h in range(NH):
                        nc.vector.tensor_scalar(skip[:, h], u[sy][:, h, b], pk(sy, "D")[:, h:h + 1], None,
                                                ALU.mult).then_inc(skip_ready, 1)
                    dve.wait_ge(c_ready, sy + 1)
                    nc.vector.tensor_copy(c_now[:], c_tok[sy][:, b]).then_inc(du_ready, 1)

                def silu_gate(j, t):
                    dve.wait_ge(tanh_done, 2 * (base + j) + t + 1)
                    nc.vector.scalar_tensor_tensor(out=silu[:, t], in0=th[:, t], scalar=1.0,
                                                   in1=ps_gu[:, t, 0:PIECE], op0=ALU.add,
                                                   op1=ALU.mult).then_inc(silu_done, 1)

                def hidden(j, t):
                    dve.wait_ge(silu_done, 2 * (base + j) + t + 1)
                    wait(dve, hid_psum, base + j)
                    for f0, f1, e in segments(my, j):
                        ins = nc.vector.scalar_tensor_tensor(
                            out=hid[:, t, f0:f1], in0=ps_gu[:, t, PIECE + f0:PIECE + f1],
                            scalar=cw[my][:, t, e:e + 1], in1=silu[:, t, f0:f1], op0=ALU.mult, op1=ALU.mult)
                    ins.then_inc(hid_done, 1)

                def times_b(q):
                    dve.wait_ge(brep_psum, NQ * k + q + 1)
                    if q == 0:
                        dve.wait_ge(du_ready, DU * (k + 1))
                    wait(dve, state_psum, NS * k + 2 * (q - 1))
                    nc.vector.tensor_tensor(
                        state[:, q % 2].rearrange("p (h i l) -> p h i l", h=NH, i=2),
                        du[:].unsqueeze(2).broadcast_to([P, NH, 2, L]),
                        ps_br[:, q % 2].rearrange("p (i l) -> p i l", i=2).unsqueeze(1).broadcast_to([P, NH, 2, L]),
                        ALU.mult).then_inc(dbu_done, 1)

                def scan(q):
                    dve.wait_ge(dbu_done, NQ * k + q + 1)
                    dve.wait_ge(decay_ready, NQ * k + q + 1)
                    nc.vector.tensor_tensor_scan(state[:, q % 2], decay[:, q % 2], state[:, q % 2], 0.0,
                                                 ALU.mult, ALU.add).then_inc(scan_done, 1)

                def times_c(q):
                    for i in range(2):
                        n = 2 * q + i
                        dve.wait_ge(state_psum, NS * k + n + 1)
                        if n == 0:
                            dve.wait_ge(acc_init, k + 1)
                        for t in range(NH):
                            if n:
                                dve.wait_ge(acc_done, 2 * NS * k + 2 * (n - 1) + t + 1)
                            nc.vector.scalar_tensor_tensor(
                                out=acc[:, t], in0=ps_ht[:, i, t * D:(t + 1) * D], scalar=c_now[:, t, n:n + 1],
                                in1=acc[:, t], op0=ALU.mult, op1=ALU.add).then_inc(acc_done, 1)

                for j in range(slots(my) + 1):
                    mon = on and j < NP[my]
                    if mon:
                        silu_gate(j, 0)
                    if son and j < NQ:
                        times_b(j)
                    if mon:
                        hidden(j, 0)
                        silu_gate(j, 1)
                    if son and j < NQ:
                        scan(j)
                    if mon:
                        hidden(j, 1)
                    if son:
                        if j == 1:
                            dve.wait_ge(x_loaded, 16)
                            if sy:
                                dve.wait_ge(x_added, b + 1)
                            hold()
                            z_norm[0]()
                        if j == 2:
                            z_norm[1]()
                        if j == 3:
                            z_norm[2]()
                        if j == 6:
                            dve.wait_ge(z_tanh, k + 1)
                            wait(dve, z_psum, k)
                            nc.vector.scalar_tensor_tensor(out=z_silu[:], in0=z_th[:], scalar=1.0, in1=zn[:],
                                                           op0=ALU.add, op1=ALU.mult).then_inc(z_silu_done, 1)
                        if 1 <= j <= NQ:
                            times_c(j - 1)
                if son:
                    dve.wait_ge(z_psum, k + 1)
                    dve.wait_ge(acc_done, 2 * NS * (k + 1))
                    nc.vector.scalar_tensor_tensor(
                        out=gated[:].rearrange("p t e -> p (t e)"), in0=acc[:].rearrange("p t e -> p (t e)"),
                        scalar=gate_f[:, sy:sy + 1], in1=ps_ht[:, 0], op0=ALU.mult,
                        op1=ALU.mult).then_inc(gated_done, 1)
                    dve.wait_ge(gated_done, k + 1)
                    nc.vector.tensor_tensor(x[:, b], x[:, b], gated[:], ALU.add).then_inc(x_gated, 1)
                    dve.wait_ge(x_gated, k + 1)
                    hold()
                    x_norm[0]()
                    x_norm[1]()
                    wait(dve, xn_psum, k)
                    x_norm[2]()
                if on:
                    bm = m - NB * my
                    dve.wait_ge(down_done, base + NP[my])
                    nc.vector.scalar_tensor_tensor(
                        out=x[:, bm].rearrange("p t e -> p (t e)"), in0=ps_out[:], scalar=gate_f[:, 2 + my:3 + my],
                        in1=x[:, bm].rearrange("p t e -> p (t e)"), op0=ALU.mult, op1=ALU.add).then_inc(x_added, 1)

            stages(dve, stage)


def kernel(**inp):
    import concourse.bacc as _bacc
    import ml_dtypes
    from concourse import mybir as _mybir
    from concourse.bass_utils import run_bass_kernel_spmd as _run

    v = {n: np.asarray(a) for n, a in inp.items()}
    zeros = np.zeros

    def halves(a):
        return a.reshape(NH, P, -1).transpose(1, 0, 2)

    def packed(y):
        g = lambda n: v[f"L{y}_xattn_{n}"]
        proj = g("x_proj_w").T
        group = np.concatenate([proj[:, :DR + NS], zeros((D, GRP - DR - NS), np.float32)], 1)
        w_dt = np.concatenate([g("dt_proj_w").T, zeros((P - DR, D), np.float32)], 0)
        parts = [halves(g("conv_b")[:, None]), halves(g("dt_proj_b")[:, None]), halves(g("D")[:, None]),
                 halves(g("A_log")), halves(np.concatenate([group] * 3, 1)), halves(proj[:, DR + NS:]),
                 g("in_proj_w").T, w_dt]
        return np.ascontiguousarray(np.concatenate([p.reshape(P, -1) for p in parts], 1))

    def expert_weights(gate, up, down):
        n = gate.shape[1] // PIECE
        w = np.stack([gate, up], 1).reshape(NH, P, 2, n, PIECE).transpose(3, 1, 0, 2, 4).reshape(n, P, -1)
        d = down.reshape(n, 2, P, D).transpose(0, 2, 1, 3).reshape(n, P, -1)
        return np.ascontiguousarray(np.concatenate([w, d], 2))

    f = lambda n: v[f"L0_ffn_{n}"]
    w0 = expert_weights(
        np.concatenate([f("wg").reshape(-1, D), f("sg")], 0).T, np.concatenate([f("wu").reshape(-1, D), f("su")], 0).T,
        np.concatenate([f("wd").transpose(0, 2, 1).reshape(-1, D), f("sd").T], 0))
    f1 = lambda n: v[f"L1_ffn_{n}"]
    flat = lambda a: a.transpose(1, 0, 2).reshape(D, -1)
    w1 = expert_weights(
        np.concatenate([flat(f1("Wu")), f1("Su")[0]], 1), np.concatenate([flat(f1("Wg")), f1("Sg")[0]], 1),
        np.concatenate([f1("Wd").reshape(-1, D), f1("Sd")[0]], 0))
    router0 = halves(np.concatenate([f("cls_w"), f("gate_w")], 0).T)
    router1 = halves(f1("router_w").T)
    ctx = np.concatenate([zeros((DCTX, NB, TAPS - 1), np.float32), v["ctx_1024"].transpose(2, 0, 1)], 2)
    convw = np.stack([v["L0_xattn_conv_w"].T.reshape(-1), v["L1_xattn_conv_w"][:, 0].T.reshape(-1)])
    const = np.concatenate([np.eye(P, dtype=np.float32), np.tile(np.arange(NS, dtype=np.float32), (P, 1))], 1)
    row = np.arange(3 * GRP) % GRP
    sel = np.repeat((row[:, None] == DR + np.arange(NS)[None, :])[:, :, None], P, 2).astype(ml_dtypes.bfloat16)
    arrays = {
        "x": v["x"].reshape(NB, NH, P, D).transpose(2, 0, 1, 3),
        "ctx": ctx, "pack0": packed(0), "pack1": packed(1), "convw": convw,
        "gates": np.concatenate([v["g_xattn"], v["g_ffn"]])[None, :],
        "weights0": w0, "weights1": w1, "router0": router0, "router1": router1,
        "rows": np.concatenate([f("extra_scale"), f("extra_bias"), f1("router_bias")])[None, :],
        "const": const, "sel": sel,
    }
    arrays = {n + "_in": np.ascontiguousarray(a) for n, a in arrays.items()}
    nc = _bacc.Bacc("TRN2", target_bir_lowering=False, num_devices=1)
    aps = {n: nc.dram_tensor(n, a.shape, _mybir.dt.from_np(a.dtype), kind="ExternalInput").ap()
           for n, a in arrays.items()}
    out = nc.dram_tensor("out", (NB, P, NH, D), _mybir.dt.float32, kind="ExternalOutput").ap()
    build(nc, aps["x_in"], aps["ctx_in"], [aps["pack0_in"], aps["pack1_in"]], aps["convw_in"], aps["gates_in"],
          [aps["weights0_in"], aps["weights1_in"]], [aps["router0_in"], aps["router1_in"]], aps["rows_in"],
          aps["const_in"], aps["sel_in"], out)
    got = _run(nc, [arrays], core_ids=[0]).results[0]["out"]
    return got.transpose(0, 2, 1, 3).reshape(NB, L, D)
```

```python
from contextlib import ExitStack

import concourse.bass as bass
from concourse import mybir
import numpy as np

F32 = mybir.dt.float32
BF16 = mybir.dt.bfloat16
F32R = mybir.dt.float32r
U32 = mybir.dt.uint32
ALU = mybir.AluOpType
ACT = mybir.ActivationFunctionType
AX_X = mybir.AxisListType.X

P = 128
NB = 4
L = 256
D = 256
DCTX = 128
NH = D // P
NS = 16
DR = 8
TAPS = 4
NQ = NS // 2
GRP = 32
EXPERTS = (14, 16)
INTER = (176, 128)
SHARED = (352, 256)
PIECE = 256
HIDDEN = tuple(EXPERTS[y] * INTER[y] + SHARED[y] for y in range(2))
NP = tuple(HIDDEN[y] // PIECE for y in range(2))
WIDE = NH * 2 * PIECE
BLOCKS = 4
BT = 2 * L
EPS = 1e-5
SMALL = 16 * 9
CONSTS = 5
ROUTER_STEPS = 16

POS = {None: list(range(NQ)), 0: list(range(0, 2 * NQ, 2)), 1: [0] + list(range(1, 2 * NQ - 1, 2))}
LAG = {None: 1, 0: 2, 1: 2}
LAST = {None: 11, 0: 2 * NP[0] + 1, 1: 2 * NP[1] + 1}
TURN_Z = {my: POS[my][-1] + LAG[my] + 1 for my in POS}
TURN_X = {my: TURN_Z[my] + 2 for my in POS}
LOGITS = {my: min(TURN_X[my] + 1, LAST[my]) for my in POS}
ROUTE = {my: min(TURN_X[my] + 2, LAST[my]) for my in POS}
PARTS = {None: TURN_X[None], 0: max(TURN_X[0], 2 * NP[0]), 1: max(TURN_X[1], 2 * NP[1])}

PK, at = {}, 0
for _name, _n in (("conv_b", NH), ("dt_b", NH), ("D", NH), ("A_log", NH * NS), ("xp", NH * 3 * GRP),
                  ("xc", NH * NS), ("w_in", D), ("w_dt", D)):
    PK[_name] = (at, at + _n)
    at += _n
PKCOLS = at
RW = (2 * EXPERTS[0], EXPERTS[1])


def pieces_before(m, y):
    return NP[0] * m if y == 0 else NP[1] * m + NB * (NP[0] - NP[1])


def segments(y, j):
    out, f = [], j * PIECE
    while f < (j + 1) * PIECE:
        e = min(f // INTER[y], EXPERTS[y])
        end = (j + 1) * PIECE if e == EXPERTS[y] else min((e + 1) * INTER[y], (j + 1) * PIECE)
        out.append((f - j * PIECE, end - j * PIECE, e))
        f = end
    return out


def wait(eng, sem, value):
    if not isinstance(value, int) or value > 0:
        eng.wait_ge(sem, value)


def build(nc, x_in, ctx_in, pack_in, convw_in, gates_in, wide_in, down_in, router_in, rows_in, const_in,
          sel_in, out):
    with ExitStack() as stack:
        def sb(name, shape, dt=F32, on=stack):
            return on.enter_context(nc.sbuf_tensor(name, shape, dt))

        def ps(name, shape):
            return stack.enter_context(nc.psum_tensor(name, shape, F32))

        def sem(name):
            return stack.enter_context(nc.semaphore(name))

        x = sb("x", [P, NB, NH, D])
        down_w = sb("down_w", [P, NP[0], 2 * D])
        wide_raw = sb("wide_raw", [P, 2, WIDE])
        ident = sb("ident", [P, P])
        iota = sb("iota", [P, NS])
        sel = sb("sel", [3 * GRP, NS], BF16)
        router_w = [sb(f"router_w{y}", [P, NH, RW[y]]) for y in range(2)]
        rows = sb("rows", [P, 2 * EXPERTS[0] + EXPERTS[1]])
        gates = sb("gates", [P, 4])
        gate_f = sb("gate_f", [P, 4])
        a_neg = sb("a_neg", [P, 2, NH, NS])
        d_col = sb("d_col", [P, 2, NH])
        minus_half = sb("minus_half", [P, NH])
        ones = sb("ones", [P, 1])
        eps = sb("eps", [P, NH])
        pause = sb("pause", [P, 1])
        u = [sb(f"u{y}", [P, NH, NB, L]) for y in range(2)]
        delta = [sb(f"delta{y}", [P, NH, NB, L]) for y in range(2)]
        bstack = [sb(f"bstack{y}", [3 * GRP, NB, L], BF16) for y in range(2)]
        c_tok = [sb(f"c_tok{y}", [P, NB, NH, NS]) for y in range(2)]
        du = sb("du", [P, NH, L])
        delta_now = sb("delta_now", [P, NH, L])
        c_now = sb("c_now", [P, NH, NS])
        decay = sb("decay", [P, 2, NH * 2 * L])
        state = sb("state", [P, 2, NH * 2 * L])
        acc = sb("acc", [P, NH, D])
        stat = [sb(f"{n}_stat", [P, NH, 6]) for n in "zx"]
        mv = [sb(f"{n}_mv", [P, NH, 2]) for n in "zx"]
        rstd = [sb(f"{n}_rstd", [P, NH]) for n in "zx"]
        normed = sb("normed", [P, NH, D])
        z_silu = sb("z_silu", [P, NH, L])
        xn_next = sb("xn_next", [P, NH, L])
        xn_hi = sb("xn_hi", [P, NH, L], F32R)
        xn_lo = sb("xn_lo", [P, NH, L], F32R)
        cw = [sb(f"cw{y}", [P, NH, EXPERTS[y] + 1]) for y in range(2)]
        lg = sb("lg", [P, NH, 32])
        r_a = sb("r_a", [P, NH, NS])
        r_b = sb("r_b", [P, NH, NS])
        r_e = sb("r_e", [P, NH, NS])
        r_one = sb("r_one", [P, NH])
        r_sum = sb("r_sum", [P, NH])
        top = sb("top", [P, NH, 8])
        top_i = sb("top_i", [P, NH, 8], U32)
        top_f = sb("top_f", [P, NH, 8])
        mask = sb("mask", [P, NH, NS])
        th = sb("th", [P, NH, PIECE])
        hid = sb("hid", [P, NH, PIECE])
        hid_t = sb("hid_t", [P, 2, 2, NH, P])
        with ExitStack() as early:
            pack = [sb(f"pack{y}", [P, PKCOLS], on=early) for y in range(2)]
            ctx_t = sb("ctx_t", [P, NB, L + TAPS - 1], on=early)
            convw = [sb(f"convw{y}", [P, TAPS, D], on=early) for y in range(2)]
            w_taps = [sb(f"w_taps{y}", [P, TAPS, D], on=early) for y in range(2)]
            half_b = sb("half_b", [P, 2, NH], on=early)
            v_th = sb("v_th", [P, NH, BT], on=early)
            v_half = sb("v_half", [P, NH, BT], on=early)
            xdbl = sb("xdbl", [3 * GRP, BT], on=early)
            rest = sb("rest", [3 * GRP, BT], on=early)
            mid = sb("mid", [3 * GRP, BT], BF16, on=early)
            sp_w = sb("sp_w", [P, BLOCKS, NH * BT], on=early)
            sp_ln = sb("sp_ln", [P, BLOCKS, NH * BT], on=early)
            sp_q = sb("sp_q", [P, NH * BT], on=early)
        wide_hl = sb("wide_hl", [P, NP[0], 2, WIDE], F32R)

        ps_gu = ps("ps_gu", [P, NH, 512])
        ps_t = ps("ps_t", [P, 512])
        ps_out = ps("ps_out", [P, 512])
        ps_br = ps("ps_br", [P, 2, 512])
        ps_ht = ps("ps_ht", [P, 2, 512])

        small_in = sem("small_in")
        rest_in = sem("rest_in")
        convw_in_s = [sem(f"convw_in{y}") for y in range(2)]
        x_loaded = sem("x_loaded")
        raw_in = [sem(f"raw_in{i}") for i in range(2)]
        down_in_s = [sem(f"down_in{j}") for j in range(NP[0])]
        stored = sem("stored")
        const_set = sem("const_set")
        edge_set = sem("edge_set")
        gate_tanh = sem("gate_tanh")
        gate_ready = sem("gate_ready")
        a_exp = sem("a_exp")
        a_ready = sem("a_ready")
        half_b_ready = sem("half_b_ready")
        taps_ready = sem("taps_ready")
        conv_psum = sem("conv_psum")
        conv_read = sem("conv_read")
        u_ready = sem("u_ready")
        xdbl_psum = sem("xdbl_psum")
        xdbl_ready = sem("xdbl_ready")
        split_step = sem("split_step")
        dt_psum = sem("dt_psum")
        dt_read = sem("dt_read")
        exp_done = sem("exp_done")
        ln_done = sem("ln_done")
        softplus_step = sem("softplus_step")
        c_psum = sem("c_psum")
        c_ready = sem("c_ready")
        now_ready = sem("now_ready")
        du_ready = sem("du_ready")
        skip_ready = sem("skip_ready")
        skip_psum = sem("skip_psum")
        acc_init = sem("acc_init")
        brep_psum = sem("brep_psum")
        dbu_done = sem("dbu_done")
        decay_ready = sem("decay_ready")
        scan_done = sem("scan_done")
        state_psum = sem("state_psum")
        acc_done = sem("acc_done")
        stat_done = [sem(f"{n}_stat_done") for n in "zx"]
        mv_done = [sem(f"{n}_mv_done") for n in "zx"]
        eps_done = [sem(f"{n}_eps_done") for n in "zx"]
        rstd_done = [sem(f"{n}_rstd_done") for n in "zx"]
        normed_done = [sem(f"{n}_normed_done") for n in "zx"]
        z_tanh = sem("z_tanh")
        z_silu_done = sem("z_silu_done")
        z_psum = sem("z_psum")
        gated_done = sem("gated_done")
        x_gated = sem("x_gated")
        xn_psum = sem("xn_psum")
        xn_next_ready = sem("xn_next_ready")
        xn_hi_ready = sem("xn_hi_ready")
        xn_lo_ready = sem("xn_lo_ready")
        wide_hi_done = sem("wide_hi_done")
        wide_lo_done = sem("wide_lo_done")
        logits_psum = sem("logits_psum")
        logits_done = sem("logits_done")
        router_tanh = sem("router_tanh")
        router_exp_in = sem("router_exp_in")
        router_exp = sem("router_exp")
        router_step = sem("router_step")
        gu_psum = sem("gu_psum")
        tanh_done = sem("tanh_done")
        silu_done = sem("silu_done")
        hid_done = sem("hid_done")
        hid_psum = sem("hid_psum")
        hid_t_ready = sem("hid_t_ready")
        down_done = sem("down_done")
        x_added = sem("x_added")

        def pk(y, name):
            a, b = PK[name]
            return pack[y][:, a:b]

        def flat(a):
            return a.rearrange("p b l -> p (b l)")

        def of_block(a, g):
            return a[:, :, 2 * (g % 2):2 * (g % 2) + 2]

        def split_at(k, half):
            if k == 0:
                return [(0, j) for j in range(3)] if half == LAST[None] else []
            if k == 1:
                j = half // 2 + 3
                return [(0, j)] if half % 2 == 0 and j < NP[0] else []
            if k == NB:
                j = half // 2 - 1
                return [(1, j)] if half % 2 == 0 and 0 <= j < NP[1] else []
            return []

        def nth_split(y, j):
            return NP[0] * y + j

        block = stack.enter_context(nc.Block())

        def stages(eng, stage):
            stage(0, None, 0)
            stage(1, 0, 0)
            with eng.Fori(2, NB) as k:
                stage(k, 0, 0)
            stage(NB, 0, 1)
            with eng.Fori(NB + 1, 2 * NB) as k:
                stage(k, 1, 1)
            stage(2 * NB, 1, None)

        @block.sync
        def _(sp):
            sp.dma_start(ctx_t[:], ctx_in).then_inc(small_in, 16)
            sp.dma_start(pack[0][:], pack_in[0]).then_inc(small_in, 16)
            for y in range(2):
                sp.dma_start(convw[y][:], convw_in[y:y + 1, :].broadcast_to([P, TAPS * D]).rearrange(
                    "p (k e) -> p k e", k=TAPS)).then_inc(convw_in_s[y], 16)
                if not y:
                    sp.dma_start(gates[:], gates_in.broadcast_to([P, 4])).then_inc(small_in, 16)
                    sp.dma_start(pack[1][:], pack_in[1]).then_inc(small_in, 16)
            sp.dma_start(sel[:], sel_in).then_inc(small_in, 16)
            sp.dma_start(ident[:], const_in[:, 0:P]).then_inc(small_in, 16)
            sp.dma_start(iota[:], const_in[:, P:P + NS]).then_inc(small_in, 16)
            for y in range(2):
                sp.dma_start(router_w[y][:], router_in[y]).then_inc(small_in, 16)
            sp.dma_start(x[:], x_in).then_inc(x_loaded, 16)
            sp.dma_start(rows[:], rows_in.broadcast_to([P, 2 * EXPERTS[0] + EXPERTS[1]])).then_inc(rest_in, 16)

            def raw(y, j):
                n = nth_split(y, j)
                if n >= 2:
                    sp.wait_ge(wide_lo_done, n - 1)
                sp.dma_start(wide_raw[:, n % 2], wide_in[y][j]).then_inc(raw_in[n % 2], 16)

            for j in range(2):
                raw(0, j)
            for j in range(NP[0]):
                sp.dma_start(down_w[:, j], down_in[0][j]).then_inc(down_in_s[j], 16)
            for j in range(2, NP[0]):
                raw(0, j)
            for j in range(NP[1]):
                raw(1, j)
                sp.wait_ge(down_done, pieces_before(NB - 1, 0) + j + 1)
                sp.dma_start(down_w[:, j], down_in[1][j]).then_inc(down_in_s[j], 16)
            for b in range(NB):
                sp.wait_ge(x_added, NB + b + 1)
                sp.dma_start(out[b], x[:, b]).then_inc(stored, 16)
            sp.wait_ge(stored, 16 * NB)

        def split_b(eng, g):
            bs = bstack[g // 2][:, 2 * (g % 2):2 * (g % 2) + 2].rearrange("p b l -> p (b l)")
            n = 4 * g
            eng.wait_ge(xdbl_ready, 2 * g + 2)
            eng.tensor_tensor(rest[:], xdbl[:], bs, ALU.subtract).then_inc(split_step, 1)
            eng.wait_ge(split_step, n + 1)
            eng.tensor_copy(mid[:], rest[:]).then_inc(split_step, 1)
            eng.wait_ge(split_step, n + 2)
            eng.tensor_copy(bs[GRP:2 * GRP], mid[GRP:2 * GRP]).then_inc(split_step, 1)
            eng.wait_ge(split_step, n + 3)
            eng.tensor_tensor(bs[2 * GRP:3 * GRP], rest[2 * GRP:3 * GRP], mid[2 * GRP:3 * GRP],
                              ALU.subtract).then_inc(split_step, 1)

        def softplus_end(eng, g):
            n = 4 * g
            w, ln, q = sp_w[:, g], sp_ln[:, g], sp_q[:]
            to = of_block(delta[g // 2], g)
            eng.wait_ge(exp_done, 1 + (g > 0))
            if g:
                eng.wait_ge(softplus_step, n)
            eng.tensor_scalar(q, w, 1.0, -1.0, ALU.add, ALU.add).then_inc(softplus_step, 1)
            eng.wait_ge(softplus_step, n + 1)
            eng.wait_ge(ln_done, 1 + (g > 0))
            eng.tensor_tensor(w, w, q, ALU.subtract).then_inc(softplus_step, 1)
            eng.wait_ge(softplus_step, n + 2)
            eng.tensor_tensor(w, ln, w, ALU.add).then_inc(softplus_step, 1)
            eng.wait_ge(softplus_step, n + 3)
            eng.wait_ge(dt_read, 2 * g + 2)
            eng.tensor_tensor(to, to, w.rearrange("p (h b l) -> p h b l", h=NH, b=2),
                              ALU.add).then_inc(softplus_step, 1)

        @block.gpsimd
        def _(pool):
            nc.gpsimd.memset(minus_half[:], -0.5).then_inc(const_set, 1)
            nc.gpsimd.memset(ones[:], 1.0).then_inc(const_set, 1)
            nc.gpsimd.memset(eps[:], EPS).then_inc(const_set, 1)
            for y in range(2):
                nc.gpsimd.memset(cw[y][:, :, EXPERTS[y]:EXPERTS[y] + 1], 0.5).then_inc(const_set, 1)
            pool.wait_ge(const_set, CONSTS)

            def inverse_std(i, k):
                pool.wait_ge(mv_done[i], NH * (k + 1))
                nc.gpsimd.tensor_tensor(rstd[i][:], mv[i][:, :, 1], eps[:], ALU.add).then_inc(eps_done[i], 1)
                pool.wait_ge(eps_done[i], k + 1)
                nc.gpsimd.tensor_tensor(rstd[i][:], rstd[i][:], minus_half[:], ALU.pow).then_inc(rstd_done[i], 1)

            def stage(k, my, sy):
                for half in range(LAST[my] + 1):
                    if isinstance(k, int):
                        if k == 0 and 3 <= half <= 5:
                            split_b(pool, half - 2)
                            pool.wait_ge(split_step, 4 * (half - 1))
                        if k == 0 and half == 8:
                            for g in range(1, BLOCKS):
                                softplus_end(pool, g)
                        for y, j in split_at(k, half):
                            n = nth_split(y, j)
                            pool.wait_ge(wide_hi_done, n + 1)
                            nc.gpsimd.tensor_tensor(wide_hl[:, j, 1], wide_raw[:, n % 2],
                                                    wide_hl[:, j, 0].bitcast(F32),
                                                    ALU.subtract).then_inc(wide_lo_done, 1)
                    if sy is not None and half == 3:
                        inverse_std(0, k)
                    if sy is not None and half == TURN_Z[my]:
                        inverse_std(1, k)

            stages(pool, stage)

        @block.scalar
        def _(act):
            act.wait_ge(small_in, SMALL)
            nc.scalar.activation(gate_f[:], gates[:], ACT.Tanh).then_inc(gate_tanh, 1)
            for y in range(2):
                nc.scalar.activation(a_neg[:, y].rearrange("p h n -> p (h n)"), pk(y, "A_log"),
                                     ACT.Exp).then_inc(a_exp, 1)
                nc.scalar.activation(half_b[:, y], pk(y, "conv_b"), ACT.Identity, scale=0.5).then_inc(half_b_ready, 1)
                nc.scalar.activation(d_col[:, y], pk(y, "D"), ACT.Identity).then_inc(half_b_ready, 1)
            act.wait_ge(half_b_ready, 4)

            def conv_out(g):
                for h in range(NH):
                    act.wait_ge(conv_psum, 2 * g + h + 1)
                    if g:
                        act.wait_ge(u_ready, 2 * (g - 1) + h + 1)
                    b = half_b[:, g // 2, h:h + 1]
                    nc.scalar.activation(v_th[:, h], ps_gu[:, h], ACT.Tanh, bias=b, scale=0.5)
                    nc.scalar.activation(v_half[:, h], ps_gu[:, h], ACT.Identity, bias=b,
                                         scale=0.5).then_inc(conv_read, 1)

            def proj_out(g):
                y = g // 2
                act.wait_ge(xdbl_psum, g + 1)
                if g:
                    act.wait_ge(dt_psum, 2 * g)
                    act.wait_ge(split_step, 4 * g)
                nc.scalar.activation(xdbl[:], ps_out[0:3 * GRP], ACT.Identity).then_inc(xdbl_ready, 1)
                nc.scalar.activation(bstack[y][:, 2 * (g % 2):2 * (g % 2) + 2].rearrange("p b l -> p (b l)"),
                                     ps_out[0:3 * GRP], ACT.Identity).then_inc(xdbl_ready, 1)
                act.wait_ge(c_psum, g + 1)
                nc.scalar.activation(c_tok[y][:, 2 * (g % 2):2 * (g % 2) + 2].rearrange("p b t n -> p (b t n)"),
                                     ps_gu[:, 0, 0:4 * NS], ACT.Identity).then_inc(c_ready, 1)
                for h in range(NH):
                    bank = ps_out if h else ps_t
                    act.wait_ge(dt_psum, 2 * g + h + 1)
                    b = pk(y, "dt_b")[:, h:h + 1]
                    nc.scalar.activation(flat(of_block(delta[y], g)[:, h]), bank[:], ACT.Relu, bias=b)
                    nc.scalar.activation(sp_w[:, g, h * BT:(h + 1) * BT], bank[:], ACT.Abs,
                                         bias=b).then_inc(dt_read, 1)

            def softplus_exp(g0, g1):
                w = sp_w[:, g0:g1].rearrange("p g f -> p (g f)")
                act.wait_ge(dt_read, 2 * g1)
                nc.scalar.activation(w, w, ACT.Exp, scale=-1.0).then_inc(exp_done, 1)

            def softplus_ln(g0, g1):
                act.wait_ge(exp_done, 1 + (g0 > 0))
                act.wait_ge(const_set, CONSTS)
                nc.scalar.activation(sp_ln[:, g0:g1].rearrange("p g f -> p (g f)"),
                                     sp_w[:, g0:g1].rearrange("p g f -> p (g f)"), ACT.Ln,
                                     bias=ones[:, 0:1]).then_inc(ln_done, 1)

            conv_out(0)
            proj_out(0)
            softplus_exp(0, 1)
            softplus_ln(0, 1)

            def decays(k, sy, q):
                wait(act, scan_done, NQ * k + q - 1)
                for h in range(NH):
                    for i in range(2):
                        o = (h * 2 + i) * L
                        ins = nc.scalar.activation(decay[:, q % 2, o + 1:o + L], delta_now[:, h, 1:L],
                                                   ACT.Exp, scale=a_neg[:, sy, h, 2 * q + i:2 * q + i + 1])
                ins.then_inc(decay_ready, 1)

            def begin(k, sy):
                b = k - NB * sy
                act.wait_ge(softplus_step, 4 if isinstance(k, int) and k == 0 else 4 * BLOCKS)
                act.wait_ge(u_ready, 2 if isinstance(k, int) and k == 0 else 2 * BLOCKS)
                wait(act, z_psum, k)
                nc.scalar.activation(delta_now[:], delta[sy][:, :, b], ACT.Identity).then_inc(now_ready, 1)
                for h in range(NH):
                    nc.scalar.activation(z_silu[:, h], u[sy][:, h, b], ACT.Identity,
                                         scale=d_col[:, sy, h:h + 1]).then_inc(skip_ready, 1)
                act.wait_ge(a_ready, 1)
                act.wait_ge(edge_set, 1)
                act.wait_ge(now_ready, k + 1)

            def stage(k, my, sy):
                m = k - 1
                on, son = my is not None, sy is not None
                base = pieces_before(m, my) if on else 0
                np_ = NP[my] if on else 0

                def tanh(j, t):
                    act.wait_ge(gu_psum, 2 * (base + j) + t + 1)
                    wait(act, hid_done, 2 * base + (2 * (j - 1) + t + 1 if j else 0))
                    nc.scalar.activation(th[:, t], ps_gu[:, t, 0:PIECE], ACT.Tanh,
                                         scale=0.5).then_inc(tanh_done, 1)

                def turn(j):
                    act.wait_ge(hid_psum, base + j + 1)
                    wait(act, down_done, base + (j - 1 if j >= 2 else 0))
                    nc.scalar.activation(hid_t[:, j % 2].rearrange("p k t n -> p (k t n)"), ps_t[:],
                                         ACT.Identity).then_inc(hid_t_ready, 1)

                if son:
                    begin(k, sy)
                for half in range(LAST[my] + 1):
                    j, t = half // 2, half % 2
                    if j < np_:
                        tanh(j, t)
                    if t == 0 and 1 <= j <= np_:
                        turn(j - 1)
                    if isinstance(k, int):
                        if k == 0 and half <= 2:
                            conv_out(half + 1)
                        if k == 0 and 3 <= half <= 5:
                            proj_out(half - 2)
                        if k == 0 and half == 6:
                            softplus_exp(1, BLOCKS)
                        if k == 0 and half == 7:
                            softplus_ln(1, BLOCKS)
                        for y, sj in split_at(k, half):
                            n = nth_split(y, sj)
                            act.wait_ge(raw_in[n % 2], 16 * (n // 2 + 1))
                            if y:
                                act.wait_ge(gu_psum, 2 * (pieces_before(NB - 1, 0) + sj + 1))
                            else:
                                act.wait_ge(softplus_step, 4 * BLOCKS)
                                act.wait_ge(split_step, 4 * BLOCKS)
                                act.wait_ge(u_ready, 2 * BLOCKS)
                                act.wait_ge(c_psum, BLOCKS)
                                act.wait_ge(dt_psum, 2 * BLOCKS)
                            nc.scalar.activation(wide_hl[:, sj, 0], wide_raw[:, n % 2],
                                                 ACT.Identity).then_inc(wide_hi_done, 1)
                    if not son:
                        continue
                    if half == 0:
                        decays(k, sy, 0)
                        act.wait_ge(skip_psum, k + 1)
                        wait(act, gated_done, k)
                        nc.scalar.activation(acc[:].rearrange("p t e -> p (t e)"), ps_ht[:, 1],
                                             ACT.Identity).then_inc(acc_init, 1)
                    for q in range(NQ - 1):
                        if POS[my][q] == half:
                            decays(k, sy, q + 1)
                    if half == 5:
                        act.wait_ge(normed_done[0], NH * (k + 1))
                        nc.scalar.activation(z_silu[:], normed[:], ACT.Tanh, scale=0.5).then_inc(z_tanh, 1)
                    if half == TURN_X[my]:
                        act.wait_ge(xn_psum, k + 1)
                        wait(act, logits_psum, k)
                        wait(act, xn_lo_ready, k)
                        nc.scalar.activation(flat(xn_next[:]), ps_ht[:, 1], ACT.Identity).then_inc(xn_next_ready, 1)
                    if half == PARTS[my]:
                        act.wait_ge(xn_next_ready, k + 1)
                        if on:
                            act.wait_ge(gu_psum, 2 * (base + np_))
                        nc.scalar.activation(xn_hi[:], xn_next[:], ACT.Identity).then_inc(xn_hi_ready, 1)
                    if half == ROUTE[my]:
                        if sy == 0:
                            act.wait_ge(logits_done, k + 1)
                            nc.scalar.activation(r_b[:, :, 0:EXPERTS[0]], lg[:, :, EXPERTS[0]:2 * EXPERTS[0]],
                                                 ACT.Tanh, scale=0.5).then_inc(router_tanh, 1)
                        act.wait_ge(router_exp_in, k + 1)
                        nc.scalar.activation(r_e[:, :, 0:EXPERTS[sy]], r_a[:, :, 0:EXPERTS[sy]],
                                             ACT.Exp).then_inc(router_exp, 1)

            stages(act, stage)

        @block.tensor
        def _(pe):
            pe.wait_ge(small_in, SMALL)

            def conv(g):
                y, b0 = g // 2, 2 * (g % 2)
                pe.wait_ge(taps_ready, y + 1)
                for h in range(NH):
                    if g:
                        pe.wait_ge(conv_read, 2 * (g - 1) + h + 1)
                    for k in range(TAPS):
                        mm = pe.matmul(ps_gu[:, h], w_taps[y][:, k, h * P:(h + 1) * P],
                                       ctx_t[:, b0:b0 + 2, k:k + L], start=(k == 0), stop=(k == TAPS - 1))
                    mm.then_inc(conv_psum, 1)

            def proj(g):
                y, b0 = g // 2, 2 * (g % 2)
                pe.wait_ge(u_ready, 2 * g + 2)
                if g:
                    pe.wait_ge(dt_read, 2 * g)
                for h in range(NH):
                    mm = pe.matmul(ps_out[0:3 * GRP], pk(y, "xp")[:, h * 3 * GRP:(h + 1) * 3 * GRP],
                                   flat(u[y][:, h, b0:b0 + 2]), start=(h == 0), stop=(h == 1))
                mm.then_inc(xdbl_psum, 1)
                pe.wait_ge(conv_read, 2 if g == 0 else 2 * BLOCKS)
                if g:
                    pe.wait_ge(c_ready, g)
                for t in range(2 * NH):
                    for h in range(NH):
                        mm = pe.matmul(ps_gu[:, 0, t * NS:(t + 1) * NS],
                                       u[y][:, h, b0 + t // 2, (t % 2) * P:(t % 2 + 1) * P],
                                       pk(y, "xc")[:, h * NS:(h + 1) * NS], start=(h == 0), stop=(h == 1))
                mm.then_inc(c_psum, 1)
                pe.wait_ge(xdbl_ready, 2 * g + 2)
                for h in range(NH):
                    pe.matmul((ps_out if h else ps_t)[:], pk(y, "w_dt")[0:GRP, h * P:(h + 1) * P], xdbl[0:GRP],
                              start=True, stop=True).then_inc(dt_psum, 1)

            conv(0)
            proj(0)

            def brep(k, sy, q):
                b = k - NB * sy
                pe.wait_ge(split_step, 4 if isinstance(k, int) and k == 0 else 4 * BLOCKS)
                wait(pe, dbu_done, NQ * k + q - 1)
                if q == 0:
                    wait(pe, logits_done, k)
                for i in range(2):
                    mm = pe.matmul(ps_br[:, q % 2, i * L:(i + 1) * L], sel[:, 2 * q + i:2 * q + i + 1].broadcast_to([3 * GRP, P]),
                                   bstack[sy][:, b, :], start=True, stop=True)
                mm.then_inc(brep_psum, 1)

            def turn_states(k, q):
                pe.wait_ge(scan_done, NQ * k + q + 1)
                for i in range(2):
                    n = 2 * q + i
                    if n >= 2:
                        pe.wait_ge(acc_done, 2 * NS * k + 2 * (n - 1))
                    elif n == 1:
                        pe.wait_ge(acc_init, k + 1)
                    else:
                        wait(pe, gated_done, k)
                    for t in range(NH):
                        for h in range(NH):
                            o = (h * 2 + i) * L + t * P
                            mm = pe.transpose(ps_ht[:, i, t * D + h * P:t * D + (h + 1) * P],
                                              state[:, q % 2, o:o + P], ident[:])
                    mm.then_inc(state_psum, 1)

            def turn4(bank, src, done):
                for t in range(NH):
                    for h in range(NH):
                        mm = pe.transpose(bank[:, t * D + h * P:t * D + (h + 1) * P],
                                          src[:, h, t * P:(t + 1) * P], ident[:])
                mm.then_inc(done, 1)

            def stage(k, my, sy):
                m = k - 1
                on, son = my is not None, sy is not None
                base = pieces_before(m, my) if on else 0
                np_ = NP[my] if on else 0

                def gate_up(j, t):
                    if j == 0 and t == 0:
                        pe.wait_ge(xn_hi_ready, m + 1)
                        pe.wait_ge(xn_lo_ready, m + 1)
                        wait(pe, hid_done, 2 * base)
                    elif j >= 1:
                        pe.wait_ge(hid_done, 2 * (base + j - 1) + t + 1)
                    toks = slice(t * P, (t + 1) * P)
                    if t == 0:
                        pe.wait_ge(wide_lo_done, nth_split(my, j) + 1)
                    prods = [(xn[:, d, toks], wide_hl[:, j, w, d * 2 * PIECE:(d + 1) * 2 * PIECE])
                             for d in range(NH) for xn, w in ((xn_hi, 0), (xn_hi, 1), (xn_lo, 0))]
                    for i, (xn, w) in enumerate(prods):
                        mm = pe.matmul(ps_gu[:, t], xn, w, start=(i == 0), stop=(i == len(prods) - 1))
                    mm.then_inc(gu_psum, 1)

                def turn(j):
                    pe.wait_ge(hid_done, 2 * (base + j) + 2)
                    wait(pe, hid_t_ready, base + j)
                    for blk in range(2):
                        for t in range(NH):
                            o = (blk * 2 + t) * P
                            mm = pe.transpose(ps_t[:, o:o + P], hid[:, t, blk * P:(blk + 1) * P], ident[:])
                    mm.then_inc(hid_psum, 1)

                def down_product(j):
                    pe.wait_ge(hid_t_ready, base + j + 1)
                    pe.wait_ge(down_in_s[j], 16 * (my + 1))
                    if j == 0:
                        wait(pe, x_added, m)
                    for t in range(NH):
                        for blk in range(2):
                            mm = pe.matmul(ps_out[:, t * D:(t + 1) * D], hid_t[:, j % 2, blk, t],
                                           down_w[:, j, blk * D:(blk + 1) * D],
                                           start=(j == 0 and blk == 0 and t == 0),
                                           stop=(j == np_ - 1 and blk == 1 and t == 1), skip_group_check=True)
                    mm.then_inc(down_done, 1)

                def of_s(half):
                    if half == 0:
                        pe.wait_ge(skip_ready, NH * (k + 1))
                        wait(pe, xn_next_ready, k)
                        turn4(ps_ht[:, 1], z_silu, skip_psum)
                        brep(k, sy, 0)
                        brep(k, sy, 1)
                    for q in range(NQ):
                        if POS[my][q] + LAG[my] == half:
                            turn_states(k, q)
                            if q + 2 < NQ:
                                brep(k, sy, q + 2)
                    if half == TURN_Z[my]:
                        pe.wait_ge(z_silu_done, k + 1)
                        pe.wait_ge(acc_done, 2 * NS * k + 2 * NS - 2)
                        turn4(ps_ht[:, 0], z_silu, z_psum)
                    if half == TURN_X[my]:
                        pe.wait_ge(normed_done[1], NH * (k + 1))
                        pe.wait_ge(acc_done, 2 * NS * (k + 1))
                        turn4(ps_ht[:, 1], normed, xn_psum)
                    if half == LOGITS[my]:
                        pe.wait_ge(xn_next_ready, k + 1)
                        pe.wait_ge(dbu_done, NQ * (k + 1))
                        for t in range(NH):
                            for d in range(NH):
                                mm = pe.matmul(ps_br[:, 0, t * 32:t * 32 + RW[sy]],
                                               xn_next[:, d, t * P:(t + 1) * P], router_w[sy][:, d],
                                               start=(d == 0), stop=(d == 1))
                        mm.then_inc(logits_psum, 1)

                for half in range(LAST[my] + 1):
                    j, t = half // 2, half % 2
                    if j < np_:
                        gate_up(j, t)
                    if t == 0 and 1 <= j <= np_:
                        turn(j - 1)
                    if son and half < LAST[my]:
                        of_s(half)
                    if t == 1 and 1 <= j <= np_:
                        down_product(j - 1)
                    if son and half == LAST[my]:
                        of_s(half)
                    if isinstance(k, int) and k == 0:
                        if half <= 2:
                            conv(half + 1)
                        if 3 <= half <= 5:
                            proj(half - 2)

            stages(pe, stage)

        @block.vector
        def _(dve):
            def taps(y):
                dve.wait_ge(convw_in_s[y], 16)
                nc.vector.tensor_tensor(w_taps[y][:], pk(y, "w_in").unsqueeze(1).broadcast_to([P, TAPS, D]),
                                        convw[y][:], ALU.mult).then_inc(taps_ready, 1)

            def silu_conv(g):
                for h in range(NH):
                    dve.wait_ge(conv_read, 2 * g + h + 1)
                    nc.vector.scalar_tensor_tensor(out=flat(of_block(u[g // 2], g)[:, h]), in0=v_th[:, h],
                                                   scalar=1.0, in1=v_half[:, h], op0=ALU.add,
                                                   op1=ALU.mult).then_inc(u_ready, 1)

            dve.wait_ge(small_in, SMALL)
            taps(0)
            nc.vector.memset(decay[:].rearrange("p s (g l) -> p (s g) l", l=L)[:, :, 0:1], 0.0).then_inc(edge_set, 1)
            dve.wait_ge(a_exp, 2)
            nc.vector.tensor_scalar(a_neg[:], a_neg[:], -1.0, None, ALU.mult).then_inc(a_ready, 1)
            dve.wait_ge(gate_tanh, 1)
            nc.vector.tensor_scalar(gate_f[:, 0:2], gate_f[:, 0:2], 0.5, None, ALU.mult).then_inc(gate_ready, 1)
            silu_conv(0)
            split_b(nc.vector, 0)
            softplus_end(nc.vector, 0)
            dve.wait_ge(const_set, CONSTS)
            dve.wait_ge(rest_in, 16)

            def hold():
                nc.vector.memset(pause[:], 0.0)

            def stats(i, k, b):
                hold()
                for t in range(NH):
                    nc.vector.bn_stats(stat[i][:, t], x[:, b, t]).then_inc(stat_done[i], 1)
                dve.wait_ge(stat_done[i], NH * (k + 1))
                hold()
                for t in range(NH):
                    nc.vector.bn_aggr(mv[i][:, t], stat[i][:, t]).then_inc(mv_done[i], 1)

            def normalise(i, k, b):
                dve.wait_ge(mv_done[i], NH * (k + 1))
                dve.wait_ge(rstd_done[i], k + 1)
                for t in range(NH):
                    nc.vector.tensor_scalar(normed[:, t], x[:, b, t], mv[i][:, t, 0:1], rstd[i][:, t:t + 1],
                                            ALU.subtract, ALU.mult).then_inc(normed_done[i], 1)

            def router(k, sy):
                ne = EXPERTS[sy]
                base = ROUTER_STEPS * k
                step = [0]

                def chain(ins):
                    step[0] += 1
                    ins.then_inc(router_step, 1)
                    dve.wait_ge(router_step, base + step[0])

                def over(a):
                    return a.unsqueeze(2).broadcast_to([P, NH, ne])

                a, e, bt = r_a[:, :, 0:ne], r_e[:, :, 0:ne], r_b[:, :, 0:ne]
                dve.wait_ge(logits_psum, k + 1)
                src = ps_br[:, 0, 0:64].rearrange("p (t n) -> p t n", t=NH)[:, :, 0:RW[sy]]
                nc.vector.tensor_copy(lg[:, :, 0:RW[sy]], src).then_inc(logits_done, 1)
                dve.wait_ge(logits_done, k + 1)
                if sy == 0:
                    dve.wait_ge(router_tanh, k + 1)
                    chain(nc.vector.scalar_tensor_tensor(out=bt, in0=bt, scalar=1.0, in1=lg[:, :, ne:2 * ne],
                                                         op0=ALU.add, op1=ALU.mult))
                    chain(nc.vector.scalar_tensor_tensor(out=bt, in0=bt, scalar=0.5, in1=lg[:, :, 0:ne],
                                                         op0=ALU.mult, op1=ALU.mult))
                    chain(nc.vector.scalar_tensor_tensor(out=bt, in0=bt, scalar=-1.0, in1=bt,
                                                         op0=ALU.mult, op1=ALU.max))
                else:
                    bt = lg[:, :, 0:ne]
                chain(nc.vector.tensor_reduce(r_one[:], bt, AX_X, ALU.max))
                nc.vector.tensor_tensor(a, bt, over(r_one[:]), ALU.subtract).then_inc(router_exp_in, 1)
                dve.wait_ge(router_exp, k + 1)
                if sy == 0:
                    chain(nc.vector.tensor_reduce(r_sum[:], e, AX_X, ALU.add))
                    chain(nc.vector.reciprocal(r_sum[:], r_sum[:]))
                    chain(nc.vector.tensor_tensor(e, e, over(r_sum[:]), ALU.mult))
                    bias, ranked = rows[:, ne:2 * ne], e
                else:
                    bias, ranked = rows[:, 2 * EXPERTS[0]:], bt
                chain(nc.vector.tensor_tensor(a, ranked, bias.unsqueeze(1).broadcast_to([P, NH, ne]), ALU.add))
                hold()
                for t in range(NH):
                    ins = nc.vector.max(top[:, t], r_a[:, t, 0:ne])
                chain(ins)
                hold()
                for t in range(NH):
                    ins = nc.vector.max_index(top_i[:, t], top[:, t], r_a[:, t, 0:ne])
                chain(ins)
                chain(nc.vector.tensor_copy(top_f[:], top_i[:]))
                for t in range(NH):
                    nc.vector.tensor_scalar(mask[:, t, 0:ne], iota[:, 0:ne], top_f[:, t, 0:1], 0.5,
                                            ALU.is_equal, ALU.mult)
                    ins = nc.vector.tensor_scalar(r_a[:, t, 0:ne], iota[:, 0:ne], top_f[:, t, 1:2], 0.5,
                                                  ALU.is_equal, ALU.mult)
                chain(ins)
                mk = mask[:, :, 0:ne]
                chain(nc.vector.tensor_tensor(mk, mk, a, ALU.add))
                if sy == 0:
                    chain(nc.vector.tensor_tensor(e, e, rows[:, 0:ne].unsqueeze(1).broadcast_to([P, NH, ne]),
                                                  ALU.mult))
                    chain(nc.vector.scalar_tensor_tensor(out=cw[0][:, :, 0:ne], in0=e, scalar=1.0, in1=mk,
                                                         op0=ALU.add, op1=ALU.mult))
                else:
                    chain(nc.vector.tensor_tensor(e, e, mk, ALU.mult))
                    chain(nc.vector.tensor_reduce(r_sum[:], e, AX_X, ALU.add))
                    chain(nc.vector.reciprocal(r_sum[:], r_sum[:]))
                    chain(nc.vector.scalar_tensor_tensor(out=cw[1][:, :, 0:ne], in0=e, scalar=0.5,
                                                         in1=over(r_sum[:]), op0=ALU.mult, op1=ALU.mult))
                dve.sem_inc(router_step, ROUTER_STEPS - step[0])

            def stage(k, my, sy):
                m = k - 1
                on, son = my is not None, sy is not None
                base = pieces_before(m, my) if on else 0
                np_ = NP[my] if on else 0
                first = isinstance(k, int) and k == 0
                if son:
                    b = k - NB * sy
                    dve.wait_ge(softplus_step, 4 if first else 4 * BLOCKS)
                    dve.wait_ge(u_ready, 2 if first else 2 * BLOCKS)
                    dve.wait_ge(c_ready, 1 if first else BLOCKS)
                    nc.vector.tensor_tensor(du[:], delta[sy][:, :, b], u[sy][:, :, b], ALU.mult).then_inc(du_ready, 1)
                    nc.vector.tensor_copy(c_now[:], c_tok[sy][:, b]).then_inc(du_ready, 1)

                def silu_gate(j, t):
                    dve.wait_ge(tanh_done, 2 * (base + j) + t + 1)
                    nc.vector.scalar_tensor_tensor(out=th[:, t], in0=th[:, t], scalar=1.0,
                                                   in1=ps_gu[:, t, 0:PIECE], op0=ALU.add,
                                                   op1=ALU.mult).then_inc(silu_done, 1)

                def hidden(j, t):
                    dve.wait_ge(silu_done, 2 * (base + j) + t + 1)
                    wait(dve, hid_psum, base + j)
                    for f0, f1, e in segments(my, j):
                        ins = nc.vector.scalar_tensor_tensor(
                            out=hid[:, t, f0:f1], in0=ps_gu[:, t, PIECE + f0:PIECE + f1],
                            scalar=cw[my][:, t, e:e + 1], in1=th[:, t, f0:f1], op0=ALU.mult, op1=ALU.mult)
                    ins.then_inc(hid_done, 1)

                def times_b(q):
                    dve.wait_ge(brep_psum, NQ * k + q + 1)
                    if q == 0:
                        dve.wait_ge(du_ready, 2 * (k + 1))
                    wait(dve, state_psum, NS * k + 2 * (q - 1))
                    nc.vector.tensor_tensor(
                        state[:, q % 2].rearrange("p (h i l) -> p h i l", h=NH, i=2),
                        du[:].unsqueeze(2).broadcast_to([P, NH, 2, L]),
                        ps_br[:, q % 2].rearrange("p (i l) -> p i l", i=2).unsqueeze(1).broadcast_to([P, NH, 2, L]),
                        ALU.mult).then_inc(dbu_done, 1)

                def scan(q):
                    dve.wait_ge(dbu_done, NQ * k + q + 1)
                    dve.wait_ge(decay_ready, NQ * k + q + 1)
                    nc.vector.tensor_tensor_scan(state[:, q % 2], decay[:, q % 2], state[:, q % 2], 0.0,
                                                 ALU.mult, ALU.add).then_inc(scan_done, 1)

                def times_c(q):
                    for i in range(2):
                        n = 2 * q + i
                        dve.wait_ge(state_psum, NS * k + n + 1)
                        if n == 0:
                            dve.wait_ge(acc_init, k + 1)
                        for t in range(NH):
                            if n:
                                dve.wait_ge(acc_done, 2 * NS * k + 2 * (n - 1) + t + 1)
                            nc.vector.scalar_tensor_tensor(
                                out=acc[:, t], in0=ps_ht[:, i, t * D:(t + 1) * D], scalar=c_now[:, t, n:n + 1],
                                in1=acc[:, t], op0=ALU.mult, op1=ALU.add).then_inc(acc_done, 1)

                def gate():
                    dve.wait_ge(z_psum, k + 1)
                    dve.wait_ge(acc_done, 2 * NS * (k + 1))
                    nc.vector.scalar_tensor_tensor(
                        out=acc[:].rearrange("p t e -> p (t e)"), in0=acc[:].rearrange("p t e -> p (t e)"),
                        scalar=gate_f[:, sy:sy + 1], in1=ps_ht[:, 0], op0=ALU.mult,
                        op1=ALU.mult).then_inc(gated_done, 1)
                    dve.wait_ge(gated_done, k + 1)
                    nc.vector.tensor_tensor(x[:, b], x[:, b], acc[:], ALU.add).then_inc(x_gated, 1)
                    dve.wait_ge(x_gated, k + 1)

                for half in range(LAST[my] + 1):
                    j, t = half // 2, half % 2
                    if j < np_:
                        silu_gate(j, t)
                    if son:
                        if half == 1:
                            dve.wait_ge(x_loaded, 16)
                            if sy:
                                dve.wait_ge(x_added, b + 1)
                            wait(dve, xn_psum, k)
                            stats(0, k, b)
                    for q in range(NQ):
                        if son and POS[my][q] == half:
                            times_b(q)
                    if j < np_:
                        hidden(j, t)
                    if first and half == 0:
                        taps(1)
                    if not son:
                        continue
                    for q in range(NQ):
                        if POS[my][q] == half:
                            scan(q)
                    if first and half <= 2:
                        silu_conv(half + 1)
                    if half == 4:
                        normalise(0, k, b)
                    if half == 6:
                        dve.wait_ge(z_tanh, k + 1)
                        nc.vector.scalar_tensor_tensor(out=z_silu[:], in0=z_silu[:], scalar=1.0, in1=normed[:],
                                                       op0=ALU.add, op1=ALU.mult).then_inc(z_silu_done, 1)
                    for q in range(NQ):
                        if POS[my][q] + LAG[my] == half:
                            times_c(q)
                    if half == TURN_Z[my]:
                        gate()
                        dve.wait_ge(z_silu_done, k + 1)
                        stats(1, k, b)
                    if half == TURN_Z[my] + 1:
                        normalise(1, k, b)
                    if half == PARTS[my]:
                        dve.wait_ge(xn_hi_ready, k + 1)
                        nc.vector.tensor_tensor(xn_lo[:], xn_next[:], xn_hi[:].bitcast(F32),
                                                ALU.subtract).then_inc(xn_lo_ready, 1)
                    if half == ROUTE[my]:
                        router(k, sy)
                if on:
                    bm = m - NB * my
                    dve.wait_ge(down_done, base + np_)
                    nc.vector.scalar_tensor_tensor(
                        out=x[:, bm].rearrange("p t e -> p (t e)"), in0=ps_out[:], scalar=gate_f[:, 2 + my:3 + my],
                        in1=x[:, bm].rearrange("p t e -> p (t e)"), op0=ALU.mult, op1=ALU.add).then_inc(x_added, 1)

            stages(dve, stage)


def kernel(**inp):
    import concourse.bacc as _bacc
    import ml_dtypes
    from concourse import mybir as _mybir
    from concourse.bass_utils import run_bass_kernel_spmd as _run

    v = {n: np.asarray(a) for n, a in inp.items()}
    zeros = np.zeros

    def halves(a):
        return a.reshape(NH, P, -1).transpose(1, 0, 2)

    def packed(y):
        g = lambda n: v[f"L{y}_xattn_{n}"]
        proj = g("x_proj_w").T
        group = np.concatenate([proj[:, :DR + NS], zeros((D, GRP - DR - NS), np.float32)], 1)
        w_dt = np.concatenate([g("dt_proj_w").T, zeros((P - DR, D), np.float32)], 0)
        parts = [halves(g("conv_b")[:, None]), halves(g("dt_proj_b")[:, None]), halves(g("D")[:, None]),
                 halves(g("A_log")), halves(np.concatenate([group] * 3, 1)), halves(proj[:, DR + NS:]),
                 g("in_proj_w").T, w_dt]
        return np.ascontiguousarray(np.concatenate([p.reshape(P, -1) for p in parts], 1))

    def expert_weights(gate, up, down):
        n = gate.shape[1] // PIECE
        w = np.stack([gate, up], 1).reshape(NH, P, 2, n, PIECE).transpose(3, 1, 0, 2, 4).reshape(n, P, -1)
        d = down.reshape(n, 2, P, D).transpose(0, 2, 1, 3).reshape(n, P, -1)
        return w, d

    f = lambda n: v[f"L0_ffn_{n}"]
    wide0, down0 = expert_weights(
        np.concatenate([f("wg").reshape(-1, D), f("sg")], 0).T, np.concatenate([f("wu").reshape(-1, D), f("su")], 0).T,
        np.concatenate([f("wd").transpose(0, 2, 1).reshape(-1, D), f("sd").T], 0))
    f1 = lambda n: v[f"L1_ffn_{n}"]
    flat = lambda a: a.transpose(1, 0, 2).reshape(D, -1)
    wide1, down1 = expert_weights(
        np.concatenate([flat(f1("Wu")), f1("Su")[0]], 1), np.concatenate([flat(f1("Wg")), f1("Sg")[0]], 1),
        np.concatenate([f1("Wd").reshape(-1, D), f1("Sd")[0]], 0))
    router0 = halves(np.concatenate([f("cls_w"), f("gate_w")], 0).T)
    router1 = halves(f1("router_w").T)
    ctx = np.concatenate([zeros((DCTX, NB, TAPS - 1), np.float32), v["ctx_1024"].transpose(2, 0, 1)], 2)
    convw = np.stack([v["L0_xattn_conv_w"].T.reshape(-1), v["L1_xattn_conv_w"][:, 0].T.reshape(-1)])
    const = np.concatenate([np.eye(P, dtype=np.float32), np.tile(np.arange(NS, dtype=np.float32), (P, 1))], 1)
    row = np.arange(3 * GRP) % GRP
    sel = (row[:, None] == DR + np.arange(NS)[None, :]).astype(ml_dtypes.bfloat16)
    arrays = {
        "x": v["x"].reshape(NB, NH, P, D).transpose(2, 0, 1, 3),
        "ctx": ctx, "pack0": packed(0), "pack1": packed(1), "convw": convw,
        "gates": np.concatenate([v["g_xattn"], v["g_ffn"]])[None, :],
        "wide0": wide0, "wide1": wide1, "down0": down0, "down1": down1, "router0": router0, "router1": router1,
        "rows": np.concatenate([f("extra_scale"), f("extra_bias"), f1("router_bias")])[None, :],
        "const": const, "sel": sel,
    }
    arrays = {n + "_in": np.ascontiguousarray(a) for n, a in arrays.items()}
    nc = _bacc.Bacc("TRN2", target_bir_lowering=False, num_devices=1)
    aps = {n: nc.dram_tensor(n, a.shape, _mybir.dt.from_np(a.dtype), kind="ExternalInput").ap()
           for n, a in arrays.items()}
    out = nc.dram_tensor("out", (NB, P, NH, D), _mybir.dt.float32, kind="ExternalOutput").ap()
    build(nc, aps["x_in"], aps["ctx_in"], [aps["pack0_in"], aps["pack1_in"]], aps["convw_in"], aps["gates_in"],
          [aps["wide0_in"], aps["wide1_in"]],
          [aps["down0_in"], aps["down1_in"]], [aps["router0_in"], aps["router1_in"]], aps["rows_in"],
          aps["const_in"], aps["sel_in"], out)
    got = _run(nc, [arrays], core_ids=[0]).results[0]["out"]
    return got.transpose(0, 2, 1, 3).reshape(NB, L, D)
```

```python
from contextlib import ExitStack

import concourse.bass as bass
from concourse import mybir
import numpy as np

F32 = mybir.dt.float32
BF16 = mybir.dt.bfloat16
F32R = mybir.dt.float32r
U32 = mybir.dt.uint32
ALU = mybir.AluOpType
ACT = mybir.ActivationFunctionType
AX_X = mybir.AxisListType.X

P = 128
NB = 4
UNITS = 2 * NB
L = 256
D = 256
DCTX = 128
NH = D // P
NS = 16
DR = 8
TAPS = 4
NQ = NS // 2
GRP = 32
EXPERTS = (14, 16)
INTER = (176, 128)
SHARED = (352, 256)
PIECE = 256
HIDDEN = tuple(EXPERTS[y] * INTER[y] + SHARED[y] for y in range(2))
NP = tuple(HIDDEN[y] // PIECE for y in range(2))
WIDE = NH * 2 * PIECE
BLOCKS = 4
BT = 2 * L
EPS = 1e-5
SMALL = 16 * 6
HID_LAG = 3
GU_BANKS = 3
CONSTS = 5
ROUTER_STEPS = 16
SP_STEPS = 4
AFTER_SOFTPLUS = 6

LAST = {"S": 13, "first": 2 * NP[0] + 1, "L0": 2 * NP[0] + 1, "L1": 2 * NP[1] + 1, "L1 last": 2 * NP[1] + 1,
        "M": 2 * NP[1] + 1}


def scans(now, ahead):
    return [(half, 0, NQ - len(now) + i) for i, half in enumerate(now)] + [
        (half, 1, i) for i, half in enumerate(ahead)]


SCAN = {"S": scans(range(NQ), []), "first": scans([0, 2, 4, 6, 8, 10, 12, 13], [17, 19, 20]),
        "L0": scans([0, 3, 6, 9, 12], [15, 18, 21]), "L1": scans([0, 2, 4, 6, 8], [12, 14, 16]),
        "L1 last": scans([0, 3, 5, 7, 9], []), "M": []}
AHEAD = 3
FETCH = {kind: [(max(half - 1, 0), ahead, q) for half, ahead, q in SCAN[kind]
                if ahead or q != AHEAD or kind in ("S", "first")] +
               [(LAST[kind], 1, AHEAD) for half, ahead, q in SCAN[kind] if (ahead, q) == (1, 0)] for kind in SCAN}
B_BY_VECTOR = {"S": [(0, q) for q in range(NQ)], "first": [(0, 0), (0, 1), (0, 2), (0, 6), (0, 7)], "L0": [],
               "L1": [], "L1 last": [], "M": []}
WEIGH = {kind: [(half + (kind != "S"), ahead, q) for half, ahead, q in SCAN[kind]] for kind in SCAN}
LAG = {"S": 1, "first": 3, "L0": 2, "L1": 3, "L1 last": 3, "M": 0}
SUM = {kind: [(half + LAG[kind], ahead, q) for half, ahead, q in SCAN[kind]] for kind in SCAN}
GATE = {kind: max([half for half, ahead, q in SUM[kind] if not ahead] + [0]) for kind in SCAN}
TO_TURN = {"S": 1, "first": 2, "L0": 2, "L1": 2, "L1 last": 2, "M": 0}
TURN_Y = {kind: GATE[kind] + TO_TURN[kind] for kind in SCAN}
TURN_X = {kind: TURN_Y[kind] + 2 for kind in SCAN}
LOGITS = {kind: TURN_X[kind] + 1 for kind in SCAN}
ROUTE = {kind: LOGITS[kind] + (kind != "S") for kind in SCAN}
BEGIN = {kind: GATE[kind] - 1 if (SCAN[kind] and SCAN[kind][-1][1]) else None for kind in SCAN}
PARTS = {"S": TURN_X["S"], "first": 2 * NP[0] - 1, "L0": 2 * NP[0] - 1, "L1": 2 * NP[1] - 1,
         "L1 last": 2 * NP[1] - 1, "M": None}

PREP = {0: [("conv", 1, 1)], 1: [("conv", 2, 0)], 2: [("proj", 1, 0)], 3: [("conv", 2, 1), ("dt", 1, 0)],
        4: [("conv", 3, 0)], 5: [("proj", 2, 0)], 6: [("conv", 3, 1), ("dt", 2, 0)], 8: [("proj", 3, 0)],
        9: [("dt", 3, 0)]}
EXP_AT, LN_AT = (0, 10), (0, LAST["S"])
SOFTPLUS_OUT = {(1, 2 * (g - 1) + i): [(g, (2 * i, 2 * i + 1))] for g in (1, 2, 3) for i in (0, 1)}
SPLIT_0 = {4: [(0, 0)], 7: [(0, 1)], 11: [(0, 2)]}
SPLIT_1 = {0: [(0, 3)], 2: [(0, 4)], 4: [(0, 5)], 7: [(0, 6)], 9: [(0, 7)], 11: [(0, 8)], 13: [(0, 9)],
           15: [(0, 10)]}

PK, at = {}, 0
for _name, _n in (("conv_b", NH), ("dt_b", NH), ("D", NH), ("A_log", NH * NS), ("xp", NH * P),
                  ("w_in", D), ("w_dt", D)):
    PK[_name] = (at, at + _n)
    at += _n
PKCOLS = at
RW = (2 * EXPERTS[0], EXPERTS[1])


def pieces_before(m, y):
    return NP[0] * m if y == 0 else NP[1] * m + NB * (NP[0] - NP[1])


def segments(y, j):
    out, f = [], j * PIECE
    while f < (j + 1) * PIECE:
        e = min(f // INTER[y], EXPERTS[y])
        end = (j + 1) * PIECE if e == EXPERTS[y] else min((e + 1) * INTER[y], (j + 1) * PIECE)
        out.append((f - j * PIECE, end - j * PIECE, e))
        f = end
    return out


def wait(eng, sem, value):
    if not isinstance(value, int) or value > 0:
        eng.wait_ge(sem, value)


def build(nc, x_in, ctx_in, pack_in, convw_in, gates_in, wide_in, down_in, router_in, rows_in, const_in,
          sel_in, out):
    with ExitStack() as stack:
        def sb(name, shape, dt=F32, on=stack):
            return on.enter_context(nc.sbuf_tensor(name, shape, dt))

        def ps(name, shape):
            return stack.enter_context(nc.psum_tensor(name, shape, F32))

        def sem(name):
            return stack.enter_context(nc.semaphore(name))

        x = sb("x", [P, NB, NH, D])
        down_w = sb("down_w", [P, NP[0], 2 * D])
        ident = sb("ident", [P, P])
        iota = sb("iota", [P, NS])
        sel = sb("sel", [P, 2 * NS], BF16)
        router_w = [sb(f"router_w{y}", [P, NH, RW[y]]) for y in range(2)]
        rows = sb("rows", [P, 2 * EXPERTS[0] + EXPERTS[1]])
        gates = sb("gates", [P, 4])
        gate_f = sb("gate_f", [P, 4])
        a_neg = sb("a_neg", [P, UNITS, NH, NS])
        d_col = sb("d_col", [P, UNITS, NH])
        minus_half = sb("minus_half", [P, NH])
        ones = sb("ones", [P, 1])
        eps = sb("eps", [P, NH])
        pause = sb("pause", [P, 1])
        u = sb("u", [P, NH, UNITS, L])
        delta = sb("delta", [P, NH, UNITS, L])
        bstack = sb("bstack", [P, UNITS, L], BF16)
        du = sb("du", [P, NH, L])
        a_now = sb("a_now", [P, NH, NS])
        decay = sb("decay", [P, 2, NH * 2 * L])
        state = sb("state", [P, 2, NH * 2 * L])
        b_now = sb("b_now", [P, 2, 2, L])
        c_now = sb("c_now", [P, 2, 2, L])
        acc = sb("acc", [P, NH, L])
        stat = [sb(f"{n}_stat", [P, NH, 6]) for n in "zx"]
        mv = [sb(f"{n}_mv", [P, NH, 2]) for n in "zx"]
        rstd = [sb(f"{n}_rstd", [P, NH]) for n in "zx"]
        normed = sb("normed", [P, NH, D])
        z_silu = sb("z_silu", [P, NH, L])
        xn_next = sb("xn_next", [P, NH, L])
        xn_hi = sb("xn_hi", [P, NH, L], F32R)
        xn_lo = sb("xn_lo", [P, NH, L], F32R)
        cw = [sb(f"cw{y}", [P, NH, EXPERTS[y] + 1]) for y in range(2)]
        cw_next = sb("cw_next", [P, NH, max(EXPERTS)])
        lg = sb("lg", [P, NH, 32])
        r_a = sb("r_a", [P, NH, NS])
        r_b = sb("r_b", [P, NH, NS])
        r_e = sb("r_e", [P, NH, NS])
        r_one = sb("r_one", [P, NH])
        r_sum = sb("r_sum", [P, NH])
        top = sb("top", [P, NH, 8])
        top_i = sb("top_i", [P, NH, 8], U32)
        top_f = sb("top_f", [P, NH, 8])
        mask = sb("mask", [P, NH, NS])
        th = sb("th", [P, NH, PIECE])
        hid = sb("hid", [P, 2, NH, PIECE])
        hid_t = sb("hid_t", [P, 2, NH, P])
        with ExitStack() as early:
            sb("place0", [P, 2 * WIDE], on=early)
            convw = [sb(f"convw{y}", [P, TAPS, D], on=early) for y in range(2)]
            w_taps = [sb(f"w_taps{y}", [P, TAPS, D], on=early) for y in range(2)]
            v_th = sb("v_th", [P, NH, BT], on=early)
            v_half = sb("v_half", [P, NH, BT], on=early)
            ctx_t = sb("ctx_t", [P, NB, L + TAPS - 1], on=early)
            pack = [sb(f"pack{y}", [P, PKCOLS], on=early) for y in range(2)]
            half_b = sb("half_b", [P, 2, NH], on=early)
            xdbl = sb("xdbl", [P, BT], on=early)
            rest = sb("rest", [P, BT], on=early)
            mid = sb("mid", [P, BT], BF16, on=early)
            sb("to_place6", [P, 4 * WIDE - NB * (L + TAPS - 1) - 2 * PKCOLS - 2 * NH - 5 * BT // 2], on=early)
            sp_q = sb("sp_q", [P, NH * BT], on=early)
            sp_w = sb("sp_w", [P, BLOCKS, NH * BT], on=early)
            sp_ln = sb("sp_ln", [P, BLOCKS, NH * BT], on=early)
        with ExitStack() as same_place:
            wide_raw = sb("wide_raw", [P, NP[0], 2, WIDE], on=same_place)
        wide_hl = sb("wide_hl", [P, NP[0], 2, WIDE], F32R)

        ps_gu = ps("ps_gu", [P, GU_BANKS, 512])
        ps_t = ps("ps_t", [P, 512])
        ps_out = ps("ps_out", [P, 512])
        ps_b = ps("ps_b", [P, 512])
        ps_c = ps("ps_c", [P, 512])
        ps_x = ps("ps_x", [P, 512])

        small_in = sem("small_in")
        rest_in = sem("rest_in")
        convw_in_s = [sem(f"convw_in{y}") for y in range(2)]
        x_loaded = sem("x_loaded")
        pack_in_s = [sem(f"pack_in{y}") for y in range(2)]
        ctx_in_s = [sem(f"ctx_in{i}") for i in range(2)]
        raw_in = [sem(f"raw_in{j}") for j in range(NP[0])]
        down_in_s = [sem(f"down_in{j}") for j in range(NP[0])]
        stored = sem("stored")
        const_set = sem("const_set")
        edge_set = sem("edge_set")
        gate_tanh = sem("gate_tanh")
        gate_ready = sem("gate_ready")
        a_exp = sem("a_exp")
        a_ready = sem("a_ready")
        half_b_ready = sem("half_b_ready")
        taps_ready = sem("taps_ready")
        conv_psum = sem("conv_psum")
        conv_read = sem("conv_read")
        u_ready = sem("u_ready")
        xdbl_psum = sem("xdbl_psum")
        xdbl_ready = sem("xdbl_ready")
        split_step = sem("split_step")
        dt_psum = sem("dt_psum")
        dt_read = sem("dt_read")
        exp_done = sem("exp_done")
        ln_done = sem("ln_done")
        softplus_step = sem("softplus_step")
        a_now_ready = sem("a_now_ready")
        du_ready = sem("du_ready")
        acc_init = sem("acc_init")
        brep_psum = sem("brep_psum")
        b_copied = sem("b_copied")
        crep_psum = sem("crep_psum")
        c_copied = sem("c_copied")
        weighted = sem("weighted")
        dbu_done = sem("dbu_done")
        decay_ready = sem("decay_ready")
        scan_done = sem("scan_done")
        acc_first = sem("acc_first")
        acc_done = sem("acc_done")
        stat_done = [sem(f"{n}_stat_done") for n in "zx"]
        mv_done = [sem(f"{n}_mv_done") for n in "zx"]
        eps_done = [sem(f"{n}_eps_done") for n in "zx"]
        rstd_done = [sem(f"{n}_rstd_done") for n in "zx"]
        normed_done = [sem(f"{n}_normed_done") for n in "zx"]
        z_tanh = sem("z_tanh")
        z_silu_done = sem("z_silu_done")
        gated_done = sem("gated_done")
        y_psum = sem("y_psum")
        x_gated = sem("x_gated")
        xn_psum = sem("xn_psum")
        xn_next_ready = sem("xn_next_ready")
        xn_hi_ready = sem("xn_hi_ready")
        xn_lo_ready = sem("xn_lo_ready")
        wide_hi_done = sem("wide_hi_done")
        wide_lo_done = sem("wide_lo_done")
        logits_psum = sem("logits_psum")
        logits_done = sem("logits_done")
        router_tanh = sem("router_tanh")
        router_exp_in = sem("router_exp_in")
        router_exp = sem("router_exp")
        router_step = sem("router_step")
        cw_ready = sem("cw_ready")
        gu_psum = sem("gu_psum")
        tanh_done = sem("tanh_done")
        silu_done = sem("silu_done")
        hid_done = sem("hid_done")
        hid_psum = sem("hid_psum")
        hid_t_ready = sem("hid_t_ready")
        down_done = sem("down_done")
        x_added = sem("x_added")

        def pk(y, name):
            a, b = PK[name]
            return pack[y][:, a:b]

        def flat(a):
            return a.rearrange("p b l -> p (b l)")

        def of_block(a, g):
            return a[:, :, 2 * g:2 * g + 2]

        def split_at(k, half):
            at = {0: SPLIT_0, 1: SPLIT_1, NB: {2 * j + 5: [(1, j)] for j in range(NP[1])}}
            return at[k].get(half, []) if k in at else []

        def blocks_for(k):
            return 1 if isinstance(k, int) and k < 2 else BLOCKS

        def nth_split(y, j):
            return NP[0] * y + j

        block = stack.enter_context(nc.Block())

        def times_b(eng, s, q):
            if isinstance(s, int) and s == 0:
                eng.wait_ge(brep_psum, q + 1)
                b = b_bank(s, q).rearrange("p (i l) -> p i l", i=2)
            else:
                eng.wait_ge(b_copied, NQ * (s - 1) + q + 1)
                b = b_now[:, q % 2]
            if q == 0:
                eng.wait_ge(du_ready, s + 1)
            wait(eng, acc_done, NQ * s + q - 1)
            eng.tensor_tensor(
                state[:, q % 2].rearrange("p (h i l) -> p h i l", h=NH, i=2),
                du[:].unsqueeze(2).broadcast_to([P, NH, 2, L]),
                b.unsqueeze(1).broadcast_to([P, NH, 2, L]), ALU.mult).then_inc(dbu_done, 1)

        def b_bank(s, q):
            return ps_gu[:, 2] if isinstance(s, int) and s == 0 and q % 2 else ps_b[:]

        def stages(eng, stage):
            stage(0, "S", None, 0)
            stage(1, "first", 0, 0)
            with eng.Fori(2, NB) as k:
                stage(k, "L0", 0, 0)
            stage(NB, "L0", 0, 1)
            with eng.Fori(NB + 1, 2 * NB - 1) as k:
                stage(k, "L1", 1, 1)
            stage(2 * NB - 1, "L1 last", 1, 1)
            stage(2 * NB, "M", 1, None)

        def events(table, kind, half):
            return [(ahead, q) for at, ahead, q in table[kind] if at == half]

        @block.sync
        def _(sp):
            def of_block_pair(y):
                sp.dma_start(pack[y][:], pack_in[y]).then_inc(pack_in_s[y], 16)
                sp.dma_start(convw[y][:], convw_in[y:y + 1, :].broadcast_to([P, TAPS * D]).rearrange(
                    "p (k e) -> p k e", k=TAPS)).then_inc(convw_in_s[y], 16)
                sp.dma_start(ctx_t[:, 2 * y:2 * y + 2], ctx_in[:, 2 * y:2 * y + 2]).then_inc(ctx_in_s[y], 16)

            of_block_pair(0)
            sp.dma_start(gates[:], gates_in.broadcast_to([P, 4])).then_inc(small_in, 16)
            sp.dma_start(sel[:], sel_in).then_inc(small_in, 16)
            sp.dma_start(ident[:], const_in[:, 0:P]).then_inc(small_in, 16)
            sp.dma_start(iota[:], const_in[:, P:P + NS]).then_inc(small_in, 16)
            for y in range(2):
                sp.dma_start(router_w[y][:], router_in[y]).then_inc(small_in, 16)
            of_block_pair(1)
            sp.dma_start(x[:], x_in).then_inc(x_loaded, 16)
            sp.dma_start(rows[:], rows_in.broadcast_to([P, 2 * EXPERTS[0] + EXPERTS[1]])).then_inc(rest_in, 16)

            def raw(y, j):
                sp.dma_start(wide_raw[:, j, 1], wide_in[y][j]).then_inc(raw_in[j], 16)

            raw(0, 0)
            for j in range(NP[0]):
                sp.dma_start(down_w[:, j], down_in[0][j]).then_inc(down_in_s[j], 16)
            sp.wait_ge(taps_ready, 2)
            raw(0, 1)
            sp.wait_ge(conv_psum, 2 * BLOCKS)
            raw(0, 2)
            sp.wait_ge(u_ready, 2 * BLOCKS)
            raw(0, 3)
            sp.wait_ge(split_step, 4 * BLOCKS)
            sp.wait_ge(dt_read, 2 * BLOCKS)
            for j in range(4, AFTER_SOFTPLUS):
                raw(0, j)
            sp.wait_ge(softplus_step, SP_STEPS * BLOCKS)
            for j in range(AFTER_SOFTPLUS, NP[0]):
                raw(0, j)

            def down_again(j):
                sp.wait_ge(down_done, pieces_before(NB - 1, 0) + j + 1)
                sp.dma_start(down_w[:, j], down_in[1][j]).then_inc(down_in_s[j], 16)

            for j in range(NP[1]):
                sp.wait_ge(gu_psum, 2 * (pieces_before(NB - 1, 0) + j + 1))
                raw(1, j)
                if j:
                    down_again(j - 1)
            down_again(NP[1] - 1)
            for b in range(NB):
                sp.wait_ge(x_added, NB + b + 1)
                sp.dma_start(out[b], x[:, b]).then_inc(stored, 16)
            sp.wait_ge(stored, 16 * NB)

        def split_b(eng, g):
            bs = bstack[:, 2 * g:2 * g + 2].rearrange("p b l -> p (b l)")
            n = 4 * g
            eng.wait_ge(xdbl_ready, 2 * g + 2)
            eng.tensor_tensor(rest[:], xdbl[:], bs, ALU.subtract).then_inc(split_step, 1)
            eng.wait_ge(split_step, n + 1)
            eng.tensor_copy(mid[:], rest[:]).then_inc(split_step, 1)
            eng.wait_ge(split_step, n + 2)
            eng.tensor_copy(bs[2 * GRP:3 * GRP], mid[2 * GRP:3 * GRP]).then_inc(split_step, 1)
            eng.wait_ge(split_step, n + 3)
            eng.tensor_tensor(bs[3 * GRP:4 * GRP], rest[3 * GRP:4 * GRP], mid[3 * GRP:4 * GRP],
                              ALU.subtract).then_inc(split_step, 1)

        q_of = [sp_q, sp_q, sp_w[:, 0], sp_ln[:, 0]]

        def softplus_end(g, steps):
            w, ln, q = sp_w[:, g], sp_ln[:, g], q_of[g][:]
            to = of_block(delta, g)
            for i in steps:
                if i == 0:
                    nc.vector.wait_ge(exp_done, 1 + (g > 0))
                    ins = nc.vector.tensor_scalar(q, w, 1.0, -1.0, ALU.add, ALU.add)
                else:
                    nc.vector.wait_ge(softplus_step, SP_STEPS * g + i)
                if i == 1:
                    nc.vector.wait_ge(ln_done, 1 + (g > 0))
                    ins = nc.vector.tensor_tensor(w, w, q, ALU.subtract)
                if i == 2:
                    ins = nc.vector.tensor_tensor(w, ln, w, ALU.add)
                if i == 3:
                    nc.vector.wait_ge(dt_read, 2 * g + 2)
                    ins = nc.vector.tensor_tensor(to, to, w.rearrange("p (h b l) -> p h b l", h=NH, b=2), ALU.add)
                ins.then_inc(softplus_step, 1)

        @block.gpsimd
        def _(pool):
            nc.gpsimd.memset(minus_half[:], -0.5).then_inc(const_set, 1)
            nc.gpsimd.memset(ones[:], 1.0).then_inc(const_set, 1)
            nc.gpsimd.memset(eps[:], EPS).then_inc(const_set, 1)
            for y in range(2):
                nc.gpsimd.memset(cw[y][:, :, EXPERTS[y]:EXPERTS[y] + 1], 0.5).then_inc(const_set, 1)
            pool.wait_ge(const_set, CONSTS)

            def times_c(s, q):
                pool.wait_ge(scan_done, NQ * s + q + 1)
                pool.wait_ge(c_copied, NQ * s + q + 1)
                pair = state[:, q % 2].rearrange("p (h i l) -> p h i l", h=NH, i=2)
                nc.gpsimd.tensor_tensor(pair, pair, c_now[:, q % 2].unsqueeze(1).broadcast_to([P, NH, 2, L]),
                                        ALU.mult).then_inc(weighted, 1)

            def inverse_std(i, k):
                pool.wait_ge(mv_done[i], NH * (k + 1))
                nc.gpsimd.tensor_tensor(rstd[i][:], mv[i][:, :, 1], eps[:], ALU.add).then_inc(eps_done[i], 1)
                pool.wait_ge(eps_done[i], k + 1)
                nc.gpsimd.tensor_tensor(rstd[i][:], rstd[i][:], minus_half[:], ALU.pow).then_inc(rstd_done[i], 1)

            def stage(k, kind, my, sy):
                for half in range(LAST[kind] + 1):
                    for ahead, q in events(FETCH, kind, half):
                        if (ahead, q) not in B_BY_VECTOR[kind]:
                            times_b(nc.gpsimd, k + ahead, q)
                    for ahead, q in events(WEIGH, kind, half):
                        times_c(k + ahead, q)
                    if sy is not None and half == 3:
                        inverse_std(0, k)
                    if sy is not None and half == TURN_Y[kind]:
                        inverse_std(1, k)
                    if not isinstance(k, int):
                        continue
                    if k == 0:
                        for what, g, h in PREP.get(half, []):
                            if what == "proj":
                                split_b(pool, g)
                                pool.wait_ge(split_step, 4 * (g + 1))
                    for y, j in split_at(k, half):
                        pool.wait_ge(wide_hi_done, nth_split(y, j) + 1)
                        nc.gpsimd.tensor_tensor(wide_hl[:, j, 1], wide_raw[:, j, 1],
                                                wide_hl[:, j, 0].bitcast(F32),
                                                ALU.subtract).then_inc(wide_lo_done, 1)

            stages(pool, stage)

        @block.scalar
        def _(act):
            act.wait_ge(small_in, SMALL)
            for y in range(2):
                act.wait_ge(pack_in_s[y], 16)
            nc.scalar.activation(gate_f[:], gates[:], ACT.Tanh).then_inc(gate_tanh, 1)
            for y in range(2):
                units = slice(NB * y, NB * y + NB)
                nc.scalar.activation(a_neg[:, units].rearrange("p k h n -> p k (h n)"),
                                     pk(y, "A_log").unsqueeze(1).broadcast_to([P, NB, NH * NS]),
                                     ACT.Exp).then_inc(a_exp, 1)
                nc.scalar.activation(half_b[:, y], pk(y, "conv_b"), ACT.Identity, scale=0.5).then_inc(half_b_ready, 1)
                nc.scalar.activation(d_col[:, units], pk(y, "D").unsqueeze(1).broadcast_to([P, NB, NH]),
                                     ACT.Identity).then_inc(half_b_ready, 1)
            act.wait_ge(half_b_ready, 4)

            def conv_out(g, h):
                act.wait_ge(conv_psum, 2 * g + h + 1)
                if g:
                    act.wait_ge(u_ready, 2 * (g - 1) + h + 1)
                b = half_b[:, g // 2, h:h + 1]
                nc.scalar.activation(v_th[:, h], ps_gu[:, h], ACT.Tanh, bias=b, scale=0.5)
                nc.scalar.activation(v_half[:, h], ps_gu[:, h], ACT.Identity, bias=b,
                                     scale=0.5).then_inc(conv_read, 1)

            def proj_out(g):
                act.wait_ge(xdbl_psum, g + 1)
                if g:
                    act.wait_ge(dt_psum, 2 * g)
                    act.wait_ge(split_step, 4 * g)
                nc.scalar.activation(xdbl[:], ps_out[:], ACT.Identity).then_inc(xdbl_ready, 1)
                nc.scalar.activation(bstack[:, 2 * g:2 * g + 2].rearrange("p b l -> p (b l)"),
                                     ps_out[:], ACT.Identity).then_inc(xdbl_ready, 1)

            def dt_out(g):
                y = g // 2
                for h in range(NH):
                    bank = ps_out if h else ps_t
                    act.wait_ge(dt_psum, 2 * g + h + 1)
                    b = pk(y, "dt_b")[:, h:h + 1]
                    nc.scalar.activation(flat(of_block(delta, g)[:, h]), bank[:], ACT.Relu, bias=b)
                    nc.scalar.activation(sp_w[:, g, h * BT:(h + 1) * BT], bank[:], ACT.Abs,
                                         bias=b).then_inc(dt_read, 1)

            def softplus_exp(g0, g1):
                w = sp_w[:, g0:g1].rearrange("p g f -> p (g f)")
                act.wait_ge(dt_read, 2 * g1)
                nc.scalar.activation(w, w, ACT.Exp, scale=-1.0).then_inc(exp_done, 1)

            def softplus_ln(g0, g1):
                act.wait_ge(exp_done, 1 + (g0 > 0))
                act.wait_ge(const_set, CONSTS)
                nc.scalar.activation(sp_ln[:, g0:g1].rearrange("p g f -> p (g f)"),
                                     sp_w[:, g0:g1].rearrange("p g f -> p (g f)"), ACT.Ln,
                                     bias=ones[:, 0:1]).then_inc(ln_done, 1)

            for h in range(NH):
                conv_out(0, h)
            proj_out(0)
            dt_out(0)
            softplus_exp(0, 1)
            softplus_ln(0, 1)
            conv_out(1, 0)

            def decays(s, q):
                wait(act, scan_done, NQ * s + q - 1)
                if q == 0:
                    act.wait_ge(softplus_step, SP_STEPS * blocks_for(s))
                    act.wait_ge(edge_set, 1)
                    act.wait_ge(a_now_ready, s + 1)
                if not (isinstance(s, int) and s == 0):
                    copy_b(s, q)
                for h in range(NH):
                    for i in range(2):
                        o = (h * 2 + i) * L
                        ins = nc.scalar.activation(decay[:, q % 2, o + 1:o + L], delta[:, h, s, 1:L],
                                                   ACT.Exp, scale=a_now[:, h, 2 * q + i:2 * q + i + 1])
                ins.then_inc(decay_ready, 1)

            def copy_b(s, q):
                act.wait_ge(brep_psum, NQ * s + q + 1)
                wait(act, dbu_done, NQ * s + q - 1)
                nc.scalar.activation(b_now[:, q % 2].rearrange("p i l -> p (i l)"), ps_b[:],
                                     ACT.Identity).then_inc(b_copied, 1)

            def copy_c(s, q):
                act.wait_ge(crep_psum, NQ * s + q + 1)
                wait(act, weighted, NQ * s + q - 1)
                nc.scalar.activation(c_now[:, q % 2].rearrange("p i l -> p (i l)"), ps_c[:],
                                     ACT.Identity).then_inc(c_copied, 1)

            def first_sum(s):
                act.wait_ge(u_ready, 2 * blocks_for(s))
                wait(act, y_psum, s)
                for h in range(NH):
                    nc.scalar.activation(acc[:, h], u[:, h, s], ACT.Identity,
                                         scale=d_col[:, s, h:h + 1]).then_inc(acc_init, 1)

            def stage(k, kind, my, sy):
                m = k - 1
                on, son = my is not None, sy is not None
                base = pieces_before(m, my) if on else 0
                np_ = NP[my] if on else 0

                def tanh(j, t):
                    act.wait_ge(gu_psum, 2 * (base + j) + t + 1)
                    wait(act, hid_done, 2 * base + (2 * (j - 1) + t + 1 if j else 0))
                    nc.scalar.activation(th[:, t], ps_gu[:, (2 * j + t) % GU_BANKS, 0:PIECE], ACT.Tanh,
                                         scale=0.5).then_inc(tanh_done, 1)

                def turn(j):
                    act.wait_ge(hid_psum, base + j + 1)
                    wait(act, down_done, base + j)
                    nc.scalar.activation(hid_t[:].rearrange("p k t n -> p (k t n)"), ps_t[:],
                                         ACT.Identity).then_inc(hid_t_ready, 1)

                for half in range(LAST[kind] + 1):
                    j, t = half // 2, half % 2
                    if j < np_:
                        tanh(j, t)
                    for piece in range(np_):
                        if half == min(2 * piece + HID_LAG, LAST[kind]):
                            turn(piece)
                    for ahead, q in events(WEIGH, kind, half):
                        copy_c(k + ahead, q)
                    for ahead, q in events(FETCH, kind, half):
                        decays(k + ahead, q)
                    for ahead, q in events(SUM, kind, half + 1):
                        if q == 0:
                            first_sum(k + ahead)
                    if son and half == 5:
                        act.wait_ge(normed_done[0], NH * (k + 1))
                        wait(act, gated_done, k)
                        nc.scalar.activation(z_silu[:], normed[:], ACT.Tanh, scale=0.5).then_inc(z_tanh, 1)
                    if son and half == TURN_X[kind]:
                        act.wait_ge(xn_psum, k + 1)
                        wait(act, logits_psum, k)
                        wait(act, xn_lo_ready, k)
                        nc.scalar.activation(flat(xn_next[:]), ps_x[:], ACT.Identity).then_inc(xn_next_ready, 1)
                    if son and half == PARTS[kind]:
                        act.wait_ge(xn_next_ready, k + 1)
                        if on:
                            act.wait_ge(gu_psum, 2 * (base + np_))
                        nc.scalar.activation(xn_hi[:], xn_next[:], ACT.Identity).then_inc(xn_hi_ready, 1)
                    if isinstance(k, int):
                        if k == 0:
                            for what, g, h in PREP.get(half, []):
                                if what == "conv":
                                    conv_out(g, h)
                                elif what == "proj":
                                    proj_out(g)
                                else:
                                    dt_out(g)
                        if (k, half) == EXP_AT:
                            softplus_exp(1, BLOCKS)
                        if (k, half) == LN_AT:
                            softplus_ln(1, BLOCKS)
                        for y, sj in split_at(k, half):
                            act.wait_ge(raw_in[sj], 16 * (y + 1))
                            nc.scalar.activation(wide_hl[:, sj, 0], wide_raw[:, sj, 1],
                                                 ACT.Identity).then_inc(wide_hi_done, 1)
                    if not son:
                        continue
                    if half == ROUTE[kind]:
                        if sy == 0:
                            act.wait_ge(logits_done, k + 1)
                            nc.scalar.activation(r_b[:, :, 0:EXPERTS[0]], lg[:, :, EXPERTS[0]:2 * EXPERTS[0]],
                                                 ACT.Tanh, scale=0.5).then_inc(router_tanh, 1)
                        act.wait_ge(router_exp_in, k + 1)
                        nc.scalar.activation(r_e[:, :, 0:EXPERTS[sy]], r_a[:, :, 0:EXPERTS[sy]],
                                             ACT.Exp).then_inc(router_exp, 1)

            stages(act, stage)

        @block.tensor
        def _(pe):
            def conv(g, h):
                y, b0 = g // 2, 2 * (g % 2)
                pe.wait_ge(taps_ready, y + 1)
                pe.wait_ge(ctx_in_s[g % 2], 16)
                if g:
                    pe.wait_ge(conv_read, 2 * (g - 1) + h + 1)
                for k in range(TAPS):
                    mm = pe.matmul(ps_gu[:, h], w_taps[y][:, k, h * P:(h + 1) * P],
                                   ctx_t[:, b0:b0 + 2, k:k + L], start=(k == 0), stop=(k == TAPS - 1))
                mm.then_inc(conv_psum, 1)

            def proj(g):
                y = g // 2
                pe.wait_ge(u_ready, 2 * g + 2)
                pe.wait_ge(pack_in_s[y], 16)
                if g:
                    pe.wait_ge(dt_read, 2 * g)
                for h in range(NH):
                    mm = pe.matmul(ps_out[:], pk(y, "xp")[:, h * P:(h + 1) * P],
                                   flat(of_block(u, g)[:, h]), start=(h == 0), stop=(h == 1))
                mm.then_inc(xdbl_psum, 1)

            def dt(g):
                pe.wait_ge(xdbl_ready, 2 * g + 2)
                for h in range(NH):
                    pe.matmul((ps_out if h else ps_t)[:], pk(g // 2, "w_dt")[0:GRP, h * P:(h + 1) * P], xdbl[0:GRP],
                              start=True, stop=True).then_inc(dt_psum, 1)

            for h in range(NH):
                conv(0, h)
            proj(0)
            dt(0)
            conv(1, 0)
            pe.wait_ge(small_in, SMALL)

            def brep(s, q):
                pe.wait_ge(split_step, 4 * blocks_for(s))
                if isinstance(s, int) and s == 0:
                    wait(pe, dbu_done, q - 1)
                elif q == 0 and isinstance(s, int) and s == 1:
                    pe.wait_ge(dbu_done, NQ)
                else:
                    wait(pe, b_copied, NQ * (s - 1) + q)
                for i in range(2):
                    mm = pe.matmul(b_bank(s, q)[:, i * L:(i + 1) * L],
                                   sel[:, 2 * q + i:2 * q + i + 1].broadcast_to([P, P]),
                                   bstack[:, s, :], start=True, stop=True)
                mm.then_inc(brep_psum, 1)

            def crep(s, q):
                pe.wait_ge(split_step, 4 * blocks_for(s))
                wait(pe, c_copied, NQ * s + q)
                for i in range(2):
                    n = NS + 2 * q + i
                    mm = pe.matmul(ps_c[:, i * L:(i + 1) * L], sel[:, n:n + 1].broadcast_to([P, P]),
                                   bstack[:, s, :], start=True, stop=True)
                mm.then_inc(crep_psum, 1)

            def turn4(bank, src, done):
                for t in range(NH):
                    for h in range(NH):
                        mm = pe.transpose(bank[:, t * D + h * P:t * D + (h + 1) * P],
                                          src[:, h, t * P:(t + 1) * P], ident[:])
                mm.then_inc(done, 1)

            def stage(k, kind, my, sy):
                m = k - 1
                on, son = my is not None, sy is not None
                base = pieces_before(m, my) if on else 0
                np_ = NP[my] if on else 0

                def gate_up(j, t):
                    if j == 0 and t == 0:
                        pe.wait_ge(xn_hi_ready, m + 1)
                        pe.wait_ge(xn_lo_ready, m + 1)
                        wait(pe, hid_done, 2 * base)
                    elif isinstance(k, int) and k == 1 and 2 * j + t == 2:
                        pe.wait_ge(dbu_done, NQ)
                    elif 2 * j + t >= GU_BANKS:
                        pe.wait_ge(hid_done, 2 * (base + j) + t + 1 - GU_BANKS)
                    toks = slice(t * P, (t + 1) * P)
                    if t == 0:
                        pe.wait_ge(wide_lo_done, nth_split(my, j) + 1)
                    prods = [(xn[:, d, toks], wide_hl[:, j, w, d * 2 * PIECE:(d + 1) * 2 * PIECE])
                             for d in range(NH) for xn, w in ((xn_hi, 0), (xn_hi, 1), (xn_lo, 0))]
                    for i, (xn, w) in enumerate(prods):
                        mm = pe.matmul(ps_gu[:, (2 * j + t) % GU_BANKS], xn, w, start=(i == 0), stop=(i == len(prods) - 1))
                    mm.then_inc(gu_psum, 1)

                def turn(j):
                    pe.wait_ge(hid_done, 2 * (base + j) + 2)
                    wait(pe, hid_t_ready, base + j)
                    for blk in range(2):
                        for t in range(NH):
                            o = (blk * 2 + t) * P
                            mm = pe.transpose(ps_t[:, o:o + P], hid[:, j % 2, t, blk * P:(blk + 1) * P], ident[:])
                    mm.then_inc(hid_psum, 1)

                def down_product(j):
                    pe.wait_ge(hid_t_ready, base + j + 1)
                    pe.wait_ge(down_in_s[j], 16 * (my + 1))
                    if j == 0:
                        wait(pe, x_added, m)
                    for t in range(NH):
                        for blk in range(2):
                            mm = pe.matmul(ps_out[:, t * D:(t + 1) * D], hid_t[:, blk, t],
                                           down_w[:, j, blk * D:(blk + 1) * D],
                                           start=(j == 0 and blk == 0 and t == 0),
                                           stop=(j == np_ - 1 and blk == 1 and t == 1), skip_group_check=True)
                    mm.then_inc(down_done, 1)

                def of_s(half):
                    for ahead, q in events(FETCH, kind, half):
                        brep(k + ahead, q)
                    for ahead, q in events(SCAN, kind, half):
                        crep(k + ahead, q)
                    if half == TURN_Y[kind]:
                        pe.wait_ge(gated_done, k + 1)
                        wait(pe, logits_done, k)
                        turn4(ps_x, acc, y_psum)
                    if half == TURN_X[kind]:
                        pe.wait_ge(normed_done[1], NH * (k + 1))
                        pe.wait_ge(x_gated, k + 1)
                        turn4(ps_x, normed, xn_psum)
                    if half == LOGITS[kind]:
                        pe.wait_ge(xn_next_ready, k + 1)
                        for t in range(NH):
                            for d in range(NH):
                                mm = pe.matmul(ps_x[:, t * 32:t * 32 + RW[sy]],
                                               xn_next[:, d, t * P:(t + 1) * P], router_w[sy][:, d],
                                               start=(d == 0), stop=(d == 1))
                        mm.then_inc(logits_psum, 1)

                for half in range(LAST[kind] + 1):
                    j, t = half // 2, half % 2
                    if j < np_:
                        gate_up(j, t)
                    for piece in range(np_):
                        if half == min(2 * piece + HID_LAG, LAST[kind]):
                            turn(piece)
                    if son:
                        of_s(half)
                    for piece in range(np_):
                        if half == min(2 * piece + HID_LAG + 1, LAST[kind]):
                            down_product(piece)
                    if isinstance(k, int) and k == 0:
                        for what, g, h in PREP.get(half, []):
                            if what == "conv":
                                conv(g, h)
                            elif what == "proj":
                                proj(g)
                            else:
                                dt(g)

            stages(pe, stage)

        @block.vector
        def _(dve):
            def taps(y):
                dve.wait_ge(convw_in_s[y], 16)
                dve.wait_ge(pack_in_s[y], 16)
                nc.vector.tensor_tensor(w_taps[y][:], pk(y, "w_in").unsqueeze(1).broadcast_to([P, TAPS, D]),
                                        convw[y][:], ALU.mult).then_inc(taps_ready, 1)

            def silu_conv(g, h):
                dve.wait_ge(conv_read, 2 * g + h + 1)
                nc.vector.scalar_tensor_tensor(out=flat(of_block(u, g)[:, h]), in0=v_th[:, h],
                                               scalar=1.0, in1=v_half[:, h], op0=ALU.add,
                                               op1=ALU.mult).then_inc(u_ready, 1)

            taps(0)
            nc.vector.memset(decay[:].rearrange("p s (g l) -> p (s g) l", l=L)[:, :, 0:1], 0.0).then_inc(edge_set, 1)
            dve.wait_ge(a_exp, 2)
            nc.vector.tensor_scalar(a_neg[:], a_neg[:], -1.0, None, ALU.mult).then_inc(a_ready, 1)
            dve.wait_ge(gate_tanh, 1)
            nc.vector.tensor_scalar(gate_f[:, 0:2], gate_f[:, 0:2], 0.5, None, ALU.mult).then_inc(gate_ready, 1)
            for h in range(NH):
                silu_conv(0, h)
            split_b(nc.vector, 0)
            softplus_end(0, range(SP_STEPS))
            dve.wait_ge(gate_ready, 1)
            dve.wait_ge(const_set, CONSTS)
            dve.wait_ge(rest_in, 16)

            def hold():
                nc.vector.memset(pause[:], 0.0)

            def stats(i, k, b):
                hold()
                for t in range(NH):
                    nc.vector.bn_stats(stat[i][:, t], x[:, b, t]).then_inc(stat_done[i], 1)
                dve.wait_ge(stat_done[i], NH * (k + 1))
                hold()
                for t in range(NH):
                    nc.vector.bn_aggr(mv[i][:, t], stat[i][:, t]).then_inc(mv_done[i], 1)

            def normalise(i, k, b):
                dve.wait_ge(mv_done[i], NH * (k + 1))
                dve.wait_ge(rstd_done[i], k + 1)
                for t in range(NH):
                    nc.vector.tensor_scalar(normed[:, t], x[:, b, t], mv[i][:, t, 0:1], rstd[i][:, t:t + 1],
                                            ALU.subtract, ALU.mult).then_inc(normed_done[i], 1)

            def router(k, sy, part):
                ne = EXPERTS[sy]
                base = ROUTER_STEPS * k
                step = [0 if part == 0 else (1, 4)[sy == 0]]

                def chain(ins):
                    step[0] += 1
                    ins.then_inc(router_step, 1)
                    dve.wait_ge(router_step, base + step[0])

                def over(a):
                    return a.unsqueeze(2).broadcast_to([P, NH, ne])

                a, e, bt = r_a[:, :, 0:ne], r_e[:, :, 0:ne], r_b[:, :, 0:ne]
                if sy:
                    bt = lg[:, :, 0:ne]
                if part == 0:
                    dve.wait_ge(logits_psum, k + 1)
                    src = ps_x[:, 0:64].rearrange("p (t n) -> p t n", t=NH)[:, :, 0:RW[sy]]
                    nc.vector.tensor_copy(lg[:, :, 0:RW[sy]], src).then_inc(logits_done, 1)
                    dve.wait_ge(logits_done, k + 1)
                    if sy == 0:
                        dve.wait_ge(router_tanh, k + 1)
                        chain(nc.vector.scalar_tensor_tensor(out=bt, in0=bt, scalar=1.0, in1=lg[:, :, ne:2 * ne],
                                                             op0=ALU.add, op1=ALU.mult))
                        chain(nc.vector.scalar_tensor_tensor(out=bt, in0=bt, scalar=0.5, in1=lg[:, :, 0:ne],
                                                             op0=ALU.mult, op1=ALU.mult))
                        chain(nc.vector.scalar_tensor_tensor(out=bt, in0=bt, scalar=-1.0, in1=bt,
                                                             op0=ALU.mult, op1=ALU.max))
                    chain(nc.vector.tensor_reduce(r_one[:], bt, AX_X, ALU.max))
                    nc.vector.tensor_tensor(a, bt, over(r_one[:]), ALU.subtract).then_inc(router_exp_in, 1)
                    return
                dve.wait_ge(router_exp, k + 1)
                if sy == 0:
                    chain(nc.vector.tensor_reduce(r_sum[:], e, AX_X, ALU.add))
                    chain(nc.vector.reciprocal(r_sum[:], r_sum[:]))
                    chain(nc.vector.tensor_tensor(e, e, over(r_sum[:]), ALU.mult))
                    bias, ranked = rows[:, ne:2 * ne], e
                else:
                    bias, ranked = rows[:, 2 * EXPERTS[0]:], bt
                chain(nc.vector.tensor_tensor(a, ranked, bias.unsqueeze(1).broadcast_to([P, NH, ne]), ALU.add))
                hold()
                for t in range(NH):
                    ins = nc.vector.max(top[:, t], r_a[:, t, 0:ne])
                chain(ins)
                hold()
                for t in range(NH):
                    ins = nc.vector.max_index(top_i[:, t], top[:, t], r_a[:, t, 0:ne])
                chain(ins)
                chain(nc.vector.tensor_copy(top_f[:], top_i[:]))
                for t in range(NH):
                    nc.vector.tensor_scalar(mask[:, t, 0:ne], iota[:, 0:ne], top_f[:, t, 0:1], 0.5,
                                            ALU.is_equal, ALU.mult)
                    ins = nc.vector.tensor_scalar(r_a[:, t, 0:ne], iota[:, 0:ne], top_f[:, t, 1:2], 0.5,
                                                  ALU.is_equal, ALU.mult)
                chain(ins)
                mk = mask[:, :, 0:ne]
                chain(nc.vector.tensor_tensor(mk, mk, a, ALU.add))
                if sy == 0:
                    chain(nc.vector.tensor_tensor(e, e, rows[:, 0:ne].unsqueeze(1).broadcast_to([P, NH, ne]),
                                                  ALU.mult))
                    chain(nc.vector.scalar_tensor_tensor(out=cw_next[:, :, 0:ne], in0=e, scalar=1.0, in1=mk,
                                                         op0=ALU.add, op1=ALU.mult))
                else:
                    chain(nc.vector.tensor_tensor(e, e, mk, ALU.mult))
                    chain(nc.vector.tensor_reduce(r_sum[:], e, AX_X, ALU.add))
                    chain(nc.vector.reciprocal(r_sum[:], r_sum[:]))
                    chain(nc.vector.scalar_tensor_tensor(out=cw_next[:, :, 0:ne], in0=e, scalar=0.5,
                                                         in1=over(r_sum[:]), op0=ALU.mult, op1=ALU.mult))
                dve.sem_inc(router_step, ROUTER_STEPS - step[0])

            def take_weights(s, sy):
                dve.wait_ge(router_step, ROUTER_STEPS * (s + 1))
                nc.vector.tensor_copy(cw[sy][:, :, 0:EXPERTS[sy]], cw_next[:, :, 0:EXPERTS[sy]]).then_inc(cw_ready, 1)

            def begin(s):
                dve.wait_ge(softplus_step, SP_STEPS * blocks_for(s))
                dve.wait_ge(u_ready, 2 * blocks_for(s))
                wait(dve, dbu_done, NQ * s)
                nc.vector.tensor_tensor(du[:], delta[:, :, s], u[:, :, s], ALU.mult).then_inc(du_ready, 1)
                dve.wait_ge(a_ready, 1)
                wait(dve, decay_ready, NQ * s)
                nc.vector.tensor_copy(a_now[:], a_neg[:, s]).then_inc(a_now_ready, 1)

            def scan(s, q):
                dve.wait_ge(dbu_done, NQ * s + q + 1)
                dve.wait_ge(decay_ready, NQ * s + q + 1)
                nc.vector.tensor_tensor_scan(state[:, q % 2], decay[:, q % 2], state[:, q % 2], 0.0,
                                             ALU.mult, ALU.add).then_inc(scan_done, 1)

            def add_up(s, q):
                pair = state[:, q % 2].rearrange("p (h i l) -> p h i l", h=NH, i=2)
                dve.wait_ge(weighted, NQ * s + q + 1)
                if q == 0:
                    dve.wait_ge(acc_init, NH * (s + 1))
                else:
                    dve.wait_ge(acc_done, NQ * s + q)
                nc.vector.tensor_tensor(acc[:], acc[:], pair[:, :, 0], ALU.add).then_inc(acc_first, 1)
                dve.wait_ge(acc_first, NQ * s + q + 1)
                nc.vector.tensor_tensor(acc[:], acc[:], pair[:, :, 1], ALU.add).then_inc(acc_done, 1)

            def stage(k, kind, my, sy):
                m = k - 1
                on, son = my is not None, sy is not None
                base = pieces_before(m, my) if on else 0
                np_ = NP[my] if on else 0
                first = isinstance(k, int) and k == 0
                if son:
                    b = k - NB * sy

                def silu_gate(j, t):
                    dve.wait_ge(tanh_done, 2 * (base + j) + t + 1)
                    nc.vector.scalar_tensor_tensor(out=th[:, t], in0=th[:, t], scalar=1.0,
                                                   in1=ps_gu[:, (2 * j + t) % GU_BANKS, 0:PIECE], op0=ALU.add,
                                                   op1=ALU.mult).then_inc(silu_done, 1)

                def hidden(j, t):
                    dve.wait_ge(silu_done, 2 * (base + j) + t + 1)
                    if j == 0:
                        dve.wait_ge(cw_ready, m + 1)
                    wait(dve, hid_psum, base + (j - 1 if j else 0))
                    for f0, f1, e in segments(my, j):
                        ins = nc.vector.scalar_tensor_tensor(
                            out=hid[:, j % 2, t, f0:f1],
                            in0=ps_gu[:, (2 * j + t) % GU_BANKS, PIECE + f0:PIECE + f1],
                            scalar=cw[my][:, t, e:e + 1], in1=th[:, t, f0:f1], op0=ALU.mult, op1=ALU.mult)
                    ins.then_inc(hid_done, 1)

                def gate():
                    dve.wait_ge(z_silu_done, k + 1)
                    dve.wait_ge(acc_done, NQ * (k + 1))
                    nc.vector.scalar_tensor_tensor(out=acc[:], in0=acc[:], scalar=gate_f[:, sy:sy + 1],
                                                   in1=z_silu[:], op0=ALU.mult, op1=ALU.mult).then_inc(gated_done, 1)

                def update_x():
                    dve.wait_ge(y_psum, k + 1)
                    xb = x[:, b].rearrange("p t e -> p (t e)")
                    nc.vector.tensor_tensor(xb, xb, ps_x[:], ALU.add).then_inc(x_gated, 1)
                    dve.wait_ge(x_gated, k + 1)

                if kind in ("S", "first"):
                    begin(k)
                for half in range(LAST[kind] + 1):
                    j, t = half // 2, half % 2
                    if j < np_:
                        silu_gate(j, t)
                    if son:
                        if half == 1:
                            dve.wait_ge(x_loaded, 16)
                            if sy:
                                dve.wait_ge(x_added, b + 1)
                            wait(dve, xn_psum, k)
                            stats(0, k, b)
                    for ahead, q in events(SCAN, kind, half):
                        if first:
                            times_b(nc.vector, k + ahead, q)
                    if j < np_:
                        hidden(j, t)
                    if not son:
                        continue
                    for ahead, q in events(SUM, kind, half):
                        if not first:
                            add_up(k + ahead, q)
                    for ahead, q in events(SCAN, kind, half):
                        if (ahead, q) in B_BY_VECTOR[kind] and not first:
                            times_b(nc.vector, k + ahead, q)
                        scan(k + ahead, q)
                    if isinstance(k, int):
                        for g, steps in SOFTPLUS_OUT.get((k, half), []):
                            softplus_end(g, steps)
                    if first and half == 0:
                        taps(1)
                    if first and half == 0:
                        silu_conv(1, 0)
                    if first:
                        for what, g, h in PREP.get(half - 1, []):
                            if what == "conv":
                                silu_conv(g, h)
                    if half == 4:
                        normalise(0, k, b)
                    if half == 6:
                        dve.wait_ge(z_tanh, k + 1)
                        nc.vector.scalar_tensor_tensor(out=z_silu[:], in0=z_silu[:], scalar=1.0, in1=normed[:],
                                                       op0=ALU.add, op1=ALU.mult).then_inc(z_silu_done, 1)
                    for ahead, q in events(SUM, kind, half):
                        if first:
                            add_up(k + ahead, q)
                    if half == GATE[kind]:
                        gate()
                    if half == TURN_Y[kind]:
                        update_x()
                        stats(1, k, b)
                    if half == TURN_Y[kind] + 1:
                        normalise(1, k, b)
                    if half == BEGIN[kind]:
                        begin(k + 1)
                    if half == PARTS[kind]:
                        dve.wait_ge(xn_hi_ready, k + 1)
                        nc.vector.tensor_tensor(xn_lo[:], xn_next[:], xn_hi[:].bitcast(F32),
                                                ALU.subtract).then_inc(xn_lo_ready, 1)
                    if half == ROUTE[kind]:
                        router(k, sy, 0)
                    if half == ROUTE[kind] + 1:
                        router(k, sy, 1)
                    if half == max(ROUTE[kind] + 1, PARTS[kind]):
                        take_weights(k, sy)
                if on:
                    bm = m - NB * my
                    dve.wait_ge(down_done, base + np_)
                    nc.vector.scalar_tensor_tensor(
                        out=x[:, bm].rearrange("p t e -> p (t e)"), in0=ps_out[:], scalar=gate_f[:, 2 + my:3 + my],
                        in1=x[:, bm].rearrange("p t e -> p (t e)"), op0=ALU.mult, op1=ALU.add).then_inc(x_added, 1)

            stages(dve, stage)


def kernel(**inp):
    import concourse.bacc as _bacc
    import ml_dtypes
    from concourse import mybir as _mybir
    from concourse.bass_utils import run_bass_kernel_spmd as _run

    v = {n: np.asarray(a) for n, a in inp.items()}
    zeros = np.zeros

    def halves(a):
        return a.reshape(NH, P, -1).transpose(1, 0, 2)

    def packed(y):
        g = lambda n: v[f"L{y}_xattn_{n}"]
        proj = g("x_proj_w").T
        w_dt = np.concatenate([g("dt_proj_w").T, zeros((P - DR, D), np.float32)], 0)
        parts = [halves(g("conv_b")[:, None]), halves(g("dt_proj_b")[:, None]), halves(g("D")[:, None]),
                 halves(g("A_log")),
                 halves(np.concatenate([proj[:, :DR], zeros((D, GRP - DR), np.float32)] + [proj[:, DR:]] * 3, 1)),
                 g("in_proj_w").T, w_dt]
        return np.ascontiguousarray(np.concatenate([p.reshape(P, -1) for p in parts], 1))

    def expert_weights(gate, up, down):
        n = gate.shape[1] // PIECE
        w = np.stack([gate, up], 1).reshape(NH, P, 2, n, PIECE).transpose(3, 1, 0, 2, 4).reshape(n, P, -1)
        d = down.reshape(n, 2, P, D).transpose(0, 2, 1, 3).reshape(n, P, -1)
        return w, d

    f = lambda n: v[f"L0_ffn_{n}"]
    wide0, down0 = expert_weights(
        np.concatenate([f("wg").reshape(-1, D), f("sg")], 0).T, np.concatenate([f("wu").reshape(-1, D), f("su")], 0).T,
        np.concatenate([f("wd").transpose(0, 2, 1).reshape(-1, D), f("sd").T], 0))
    f1 = lambda n: v[f"L1_ffn_{n}"]
    flat = lambda a: a.transpose(1, 0, 2).reshape(D, -1)
    wide1, down1 = expert_weights(
        np.concatenate([flat(f1("Wu")), f1("Su")[0]], 1), np.concatenate([flat(f1("Wg")), f1("Sg")[0]], 1),
        np.concatenate([f1("Wd").reshape(-1, D), f1("Sd")[0]], 0))
    router0 = halves(np.concatenate([f("cls_w"), f("gate_w")], 0).T)
    router1 = halves(f1("router_w").T)
    ctx = np.concatenate([zeros((DCTX, NB, TAPS - 1), np.float32), v["ctx_1024"].transpose(2, 0, 1)], 2)
    convw = np.stack([v["L0_xattn_conv_w"].T.reshape(-1), v["L1_xattn_conv_w"][:, 0].T.reshape(-1)])
    const = np.concatenate([np.eye(P, dtype=np.float32), np.tile(np.arange(NS, dtype=np.float32), (P, 1))], 1)
    row = np.arange(P) % GRP
    sel = ((np.arange(P)[:, None] >= GRP) & (row[:, None] == np.arange(2 * NS)[None, :])).astype(ml_dtypes.bfloat16)
    arrays = {
        "x": v["x"].reshape(NB, NH, P, D).transpose(2, 0, 1, 3),
        "ctx": ctx, "pack0": packed(0), "pack1": packed(1), "convw": convw,
        "gates": np.concatenate([v["g_xattn"], v["g_ffn"]])[None, :],
        "wide0": wide0, "wide1": wide1, "down0": down0, "down1": down1, "router0": router0, "router1": router1,
        "rows": np.concatenate([f("extra_scale"), f("extra_bias"), f1("router_bias")])[None, :],
        "const": const, "sel": sel,
    }
    arrays = {n + "_in": np.ascontiguousarray(a) for n, a in arrays.items()}
    nc = _bacc.Bacc("TRN2", target_bir_lowering=False, num_devices=1)
    aps = {n: nc.dram_tensor(n, a.shape, _mybir.dt.from_np(a.dtype), kind="ExternalInput").ap()
           for n, a in arrays.items()}
    out = nc.dram_tensor("out", (NB, P, NH, D), _mybir.dt.float32, kind="ExternalOutput").ap()
    build(nc, aps["x_in"], aps["ctx_in"], [aps["pack0_in"], aps["pack1_in"]], aps["convw_in"], aps["gates_in"],
          [aps["wide0_in"], aps["wide1_in"]],
          [aps["down0_in"], aps["down1_in"]], [aps["router0_in"], aps["router1_in"]], aps["rows_in"],
          aps["const_in"], aps["sel_in"], out)
    got = _run(nc, [arrays], core_ids=[0]).results[0]["out"]
    return got.transpose(0, 2, 1, 3).reshape(NB, L, D)
```
